# Optimizing a Trainium2 kernel written in Bass

```python
import numpy as np
import jax
import jax.numpy as jnp

def _softmax(x, axis=-1):
    return jax.nn.softmax(x, axis=axis)

def _gelu(x):
    return jax.nn.gelu(x, approximate=True)

def _silu(x):
    return jax.nn.silu(x)

def _sigmoid(x):
    return jax.nn.sigmoid(x)

def _layernorm(x, axis=-1, eps=1e-05):
    m = jnp.mean(x, axis=axis, keepdims=True)
    v = jnp.var(x, axis=axis, keepdims=True)
    return (x - m) / jnp.sqrt(v + eps)

def _scatter_add(tgt, idx, src, axis=0):
    return tgt.at[idx].add(src)

def _segment_sum(src, seg, n):
    return jax.ops.segment_sum(src, seg, n)
kernel_name = 'mk_adj_ffn_d1_adj_r2_e1c5f3'

def setup_inputs(seed: int=0):
    np.random.seed(seed)
    _w = jnp.asarray

    def _rec_inputs():
        import jax
        import jax.numpy as jnp
        _gk = jax.random.key(seed)
        x = -0.0002928 + 1 * jax.random.normal(jax.random.fold_in(_gk, 1), (4096, 256), jnp.float32)
        _w = (1.0 + jnp.arange(4096, dtype=jnp.float32)) ** (-0.5)
        _w = _w / _w.mean()
        _pij = jnp.clip(0.000976562 * _w[:, None] * _w[None, :], 0.0, 1.0)
        _a = jax.random.uniform(jax.random.fold_in(_gk, 2), (4096, 4096)) < _pij
        _a = jnp.logical_or(_a, jnp.eye(4096, dtype=bool))
        _af = _a.astype(jnp.float32)
        _af = _af * jax.random.uniform(jax.random.fold_in(_gk, 3), (4096, 4096), jnp.float32, 0.05, 1)
        adj = _af
        return (x, adj)
    x, adj = _rec_inputs()

    def _L0_gnn_setup():
        import jax, jax.numpy as jnp
        import numpy as np
        N = 4096
        IN_C = 256
        OUT_C = 256
        key = jax.random.key(seed)
        k1, k2, k3 = jax.random.split(key, 3)
        x = jax.random.normal(k1, (N, IN_C), dtype=jnp.float32)
        adj = jax.random.uniform(k2, (N, N), dtype=jnp.float32)
        w = jax.random.uniform(k3, (IN_C, OUT_C), dtype=jnp.float32)
        return {'x': x, 'adj': adj, 'w': w}
    _L0_gnn_all = _L0_gnn_setup()
    _L0_gnn_in = {k: v for k, v in _L0_gnn_all.items() if k in ('w',)}
    del _L0_gnn_all

    def _L0_ffn_setup():
        import jax, jax.numpy as jnp
        import numpy as np
        B, S, H, E, K = (8, 2048, 256, 8, 2)
        key = jax.random.key(seed)
        ks = jax.random.split(key, 7)
        s_h = 1.0 / np.sqrt(H)
        s_2h = 1.0 / np.sqrt(2 * H)
        return {'x': jax.random.normal(ks[0], (B, S, H), dtype=jnp.float32), 'gate_w': jax.random.uniform(ks[1], (H, E), minval=-s_h, maxval=s_h, dtype=jnp.float32), 'gate_b': jax.random.uniform(ks[2], (E,), minval=-s_h, maxval=s_h, dtype=jnp.float32), 'w1': jax.random.uniform(ks[3], (E, H, 2 * H), minval=-s_h, maxval=s_h, dtype=jnp.float32), 'b1': jax.random.uniform(ks[4], (E, 2 * H), minval=-s_h, maxval=s_h, dtype=jnp.float32), 'w2': jax.random.uniform(ks[5], (E, 2 * H, H), minval=-s_2h, maxval=s_2h, dtype=jnp.float32), 'b2': jax.random.uniform(ks[6], (E, H), minval=-s_2h, maxval=s_2h, dtype=jnp.float32)}
    _L0_ffn_all = _L0_ffn_setup()
    _L0_ffn_in = {k: v for k, v in _L0_ffn_all.items() if k in ('gate_w', 'gate_b', 'w1', 'b1', 'w2', 'b2')}
    del _L0_ffn_all
    return {'x': x, 'adj': adj, 'L0_gnn_w': _L0_gnn_in['w'], 'L0_ffn_gate_w': _L0_ffn_in['gate_w'], 'L0_ffn_gate_b': _L0_ffn_in['gate_b'], 'L0_ffn_w1': _L0_ffn_in['w1'], 'L0_ffn_b1': _L0_ffn_in['b1'], 'L0_ffn_w2': _L0_ffn_in['w2'], 'L0_ffn_b2': _L0_ffn_in['b2']}

def reference(x, adj, L0_gnn_w, L0_ffn_gate_w, L0_ffn_gate_b, L0_ffn_w1, L0_ffn_b1, L0_ffn_w2, L0_ffn_b2):
    import jax
    import jax.numpy as jnp

    def _L0_gnn_ref(x, adj, w):
        import jax, jax.numpy as jnp
        import numpy as np
        N = 4096
        IN_C = 256
        OUT_C = 256
        A = adj + jnp.eye(adj.shape[0], dtype=adj.dtype)
        deg = jnp.sum(A, axis=1)
        d_inv_sqrt = jax.lax.rsqrt(deg)
        A_hat = A * d_inv_sqrt[:, None] * d_inv_sqrt[None, :]
        mm_1 = A_hat @ x
        return jax.nn.elu(mm_1 @ w)

    def _L0_ffn_ref(x, gate_w, gate_b, w1, b1, w2, b2):
        import jax, jax.numpy as jnp
        import numpy as np
        B, S, H, E, K = (8, 2048, 256, 8, 2)
        logits = jnp.einsum('bsh,he->bse', x, gate_w) + gate_b
        topk_vals, topk_idx = jax.lax.top_k(logits, K)
        topk_weights = jax.nn.softmax(topk_vals, axis=-1)
        mask = jax.nn.one_hot(topk_idx, E, dtype=topk_weights.dtype)
        weights = jnp.einsum('bske,bsk->bse', mask, topk_weights)
        h = jax.nn.relu(jnp.einsum('bsh,ehf->bsef', x, w1) + b1)
        expert_out = jnp.einsum('bsef,efh->bseh', h, w2) + b2
        return jnp.einsum('bseh,bse->bsh', expert_out, weights)
    x = x + _L0_gnn_ref(_layernorm(x, axis=-1), adj, L0_gnn_w)
    x = x + _L0_ffn_ref(_layernorm(x, axis=-1)[None], L0_ffn_gate_w, L0_ffn_gate_b, L0_ffn_w1, L0_ffn_b1, L0_ffn_w2, L0_ffn_b2)[0]
    return x

_drawn_inputs = setup_inputs


def setup_inputs(seed=0):
    import zlib

    import numpy as np

    out = dict(_drawn_inputs(seed))
    spreads = {}
    factors = {'L0_ffn_gate_b': 3.717, 'L0_ffn_b1': 8.0, 'L0_ffn_b2': 7.128}
    for name, (base, spread) in spreads.items():
        noise = np.random.default_rng([zlib.crc32(name.encode()), seed]).standard_normal(out[name].shape)
        drawn = base * np.exp(spread * noise) if base else spread * noise
        out[name] = jnp.asarray(drawn.astype(out[name].dtype))
    for name, factor in factors.items():
        out[name] = (out[name] * factor).astype(out[name].dtype)
    return out
```

```python
from contextlib import ExitStack

import concourse.bass as bass
from concourse import mybir

F32 = mybir.dt.float32
F32R = mybir.dt.float32r
BF16 = mybir.dt.bfloat16
I32 = mybir.dt.int32
U32 = mybir.dt.uint32
ALU = mybir.AluOpType
ACT = mybir.ActivationFunctionType
AX = mybir.AxisListType

P = 128
N = 4096
C = 256
KC = C // P
NT = N // P
BW = 512
SUB = BW // P
NB = N // BW
NPAIR = NB // 2
PT = 2 * SUB
RING = 4
YT = 2
NY = NT // YT
EPS = 1e-5

DEG, BOTH, PROD = "deg", "both", "prod"


def plan():
    steps = []
    for t in range(NPAIR):
        before = [(DEG, jp, t) for jp in range(t, NPAIR)] + [(BOTH, jp, t) for jp in range(t)]
        steps.append((before, [(PROD, t, ip) for ip in range(t + 1)]))
    return steps
E = 8
F = 512
KF = F // P
SLOTS = 2 * NT + E
PAD_ROW = 2 * N
FAR = 3.0e38
CW = 64

WIDTHS = dict(ident=P, before=P, lane=P, tile=SLOTS, expert=E, step=NT, column=CW, row=1)


def const_slices():
    at, out = 0, {}
    for name, width in WIDTHS.items():
        out[name] = slice(at, at + width)
        at += width
    return out, at


class Chain:

    def __init__(self, eng, sem):
        self.eng, self.sem, self.base, self.n = eng, sem, 0, 0

    def step(self, ins):
        self.n += 1
        ins.then_inc(self.sem, 1)
        self.eng.wait_ge(self.sem, self.base + self.n)


def in_pairs(eng, count, body, chain=None):
    start = chain.n if chain else 0
    body(0, 0)
    length = chain.n - start if chain else 0
    body(1, 1)
    assert not chain or chain.n == start + 2 * length
    with eng.Fori(1, count // 2) as i:
        for k in range(2):
            if chain:
                chain.base, chain.n = i * (2 * length), start + k * length
            body(i * 2 + k, k)
    if chain:
        chain.base, chain.n = 0, start + count * length


class Block:

    def __init__(self, n, kind, t, jp, ip, s, n_deg, n_prod):
        self.n, self.kind, self.t, self.jp, self.ip, self.s = n, kind, t, jp, ip, s
        self.j, self.strip, self.i = 2 * jp + s % 2, s // 2, 2 * ip + s // 2
        self.sums = kind != PROD
        self.multiplies = kind != DEG
        self.n_deg, self.n_prod = n_deg, n_prod


def blocks_of(steps):
    out, n, n_deg, n_prod = [], 0, 0, 0
    for t, parts in enumerate(steps):
        both = []
        for part in parts:
            row = []
            for kind, jp, ip in part:
                for s in range(4):
                    row.append(Block(n, kind, t, jp, ip, s, n_deg, n_prod))
                    n += 1
                    n_deg += kind != PROD
                    n_prod += kind != DEG
            both.append(row)
        out.append(both)
    return out


def graph_layer(nc, ctx, x, adj, w, const, consts, at_const, acc, dinv):
    steps = blocks_of(plan())
    every = [b for step in steps for part in step for b in part]
    at = {b.n: b for b in every}

    def sb(name, shape, dt=F32):
        return ctx.enter_context(nc.sbuf_tensor(name, shape, dt))

    def ps(name, shape):
        return ctx.enter_context(nc.psum_tensor(name, shape, F32))

    def sem(name):
        return ctx.enter_context(nc.semaphore(name))

    zr = sb("zr", [P, NT, C], F32R)
    zl = sb("zl", [P, NT, C], F32R)
    z = sb("z", [P, PT, C])
    raw = sb("raw", [P, RING, SUB, BW])
    ar = sb("ar", [P, 2, SUB, BW], F32R)
    al = sb("al", [P, 2, SUB, BW], F32R)
    sum_v = sb("sum_v", [P, 2, 2 * BW])
    sum_p = sb("sum_p", [P, 2, 2 * BW])
    w_raw = sb("w_raw", [P, KC, C])
    wr = sb("wr", [P, KC, C], F32R)
    wl = sb("wl", [P, KC, C], F32R)
    xin = sb("xin", [P, 2, YT, C])
    xn = sb("xn", [P, YT, C])
    xtr = sb("xtr", [P, 2, YT * C], F32R)
    xtl = sb("xtl", [P, 2, YT * C], F32R)
    ones = sb("ones", [P, 1])
    stats = sb("stats", [P, YT, 6])
    mv = sb("mv", [P, YT, 2])
    rs = sb("rs", [P, 4, YT])
    dg = sb("dg", [P, 4, PT])

    ps_prod = ps("ps_prod", [P, 2, SUB, C])
    ps_x = ps("ps_x", [P, 2, BW])
    ps_y = ps("ps_y", [P, 2, BW])

    const_loaded = sem("const_loaded")
    w_loaded = sem("w_loaded")
    ident = consts[:, at_const["ident"]]
    x_loaded = [sem(f"x_loaded{i}") for i in range(2)]
    raw_loaded = [sem(f"raw_loaded{i}") for i in range(RING)]
    ones_set = sem("ones_set")
    w_high = sem("w_high")
    w_low = sem("w_low")
    v_step = sem("v_step")
    var_inv = sem("var_inv")
    var_root = sem("var_root")
    xn_ready = sem("xn_ready")
    xt_made = sem("xt_made")
    xt_high = sem("xt_high")
    xt_low = sem("xt_low")
    y_made = sem("y_made")
    y_high = sem("y_high")
    y_low = sem("y_low")
    summed_v = sem("summed_v")
    summed_p = sem("summed_p")
    deg_made = sem("deg_made")
    deg_inv = sem("deg_inv")
    deg_root = sem("deg_root")
    z_scaled = sem("z_scaled")
    z_high = sem("z_high")
    z_low = sem("z_low")
    a_high = sem("a_high")
    a_low = sem("a_low")
    block_done = sem("block_done")
    acc_added = sem("acc_added")

    x_v = x.rearrange("(b t p) c -> b p t c", t=YT, p=P)

    block = ctx.enter_context(nc.Block())

    @block.sync
    def _(sp):
        sp.dma_start(w_raw[:, :, :], w.rearrange("(k p) c -> p k c", p=P)).then_inc(w_loaded, 16)

        def load_x(b):
            if b >= 2:
                sp.wait_ge(xn_ready, b - 1)
            sp.dma_start(xin[:, b % 2, :, :], x_v[b]).then_inc(x_loaded[b % 2], 16)

        load_x(0)
        sp.dma_start(consts[:, :], const).then_inc(const_loaded, 16)
        load_x(1)
        for b in every:
            if b.n >= RING:
                old = at[b.n - RING]
                if old.sums:
                    sp.wait_ge(summed_v, old.n_deg + 1)
                    sp.wait_ge(summed_p, old.n_deg + 1)
                if old.multiplies:
                    sp.wait_ge(a_low, old.n_prod + 1)
            sp.dma_start(raw[:, b.s, :, :], adj[b.j, b.i]).then_inc(raw_loaded[b.s], 16)
            if 2 <= b.n + 1 < NY:
                load_x(b.n + 1)

    @block.gpsimd
    def _(pool):
        pool.memset(ones[:, :], 1.0).then_inc(ones_set, 1)
        for b in every:
            if not b.sums:
                continue
            pool.wait_ge(raw_loaded[b.s], 16 * (b.n // RING + 1))
            out = sum_p[:, b.strip, :]
            src = raw[:, b.s, 2:4, :].rearrange("p s i -> p (s i)")
            if b.n_deg:
                pool.wait_ge(summed_p, b.n_deg)
            if b.jp == b.t and b.s % 2 == 0:
                if b.t:
                    pool.wait_ge(deg_made, b.t)
                pool.tensor_copy(out, src).then_inc(summed_p, 1)
            else:
                pool.tensor_tensor(out, out, src, ALU.add).then_inc(summed_p, 1)

    @block.scalar
    def _(act):
        def root(b):
            act.wait_ge(var_inv, b + 1)
            act.activation(rs[:, 1, :], rs[:, 0, :], ACT.Sqrt).then_inc(var_root, 1)

        def xt_high_part(b):
            act.wait_ge(xt_made, b + 1)
            if b >= 2:
                act.wait_ge(y_made, b - 1)
            act.activation(xtr[:, b % 2, :], ps_x[:, b % 2, :], ACT.Copy).then_inc(xt_high, 1)

        def y_high_part(b):
            act.wait_ge(y_made, b + 1)
            act.activation(zr[:, b * YT:(b + 1) * YT, :].rearrange("p t c -> p (t c)"), ps_y[:, b % 2, :],
                           ACT.Copy).then_inc(y_high, 1)

        def a_high_part(b):
            act.wait_ge(raw_loaded[b.s], 16 * (b.n // RING + 1))
            if b.n_prod >= 2:
                act.wait_ge(block_done, b.n_prod - 1)
            act.activation(ar[:, b.n_prod % 2, :, :], raw[:, b.s, :, :], ACT.Copy).then_inc(a_high, 1)

        act.wait_ge(w_loaded, 16)
        act.activation(wr[:, :, :], w_raw[:, :, :], ACT.Copy).then_inc(w_high, 1)
        for b in range(NY + 2):
            if b < NY:
                root(b)
            if 1 <= b <= NY:
                xt_high_part(b - 1)
            if b >= 2:
                y_high_part(b - 2)
        for t, (before, after) in enumerate(steps):
            for b in before:
                if b.multiplies:
                    a_high_part(b)
            act.wait_ge(deg_inv, t + 1)
            act.activation(dg[:, 2, :], dg[:, 1, :], ACT.Sqrt).then_inc(deg_root, 1)
            act.wait_ge(z_scaled, t + 1)
            act.activation(zr[:, t * PT:(t + 1) * PT, :], z[:, :, :], ACT.Copy).then_inc(z_high, 1)
            for b in after:
                a_high_part(b)

    @block.vector
    def _(dve):
        count = [0]

        def step(ins):
            count[0] += 1
            ins.then_inc(v_step, 1)
            dve.wait_ge(v_step, count[0])

        def newton(out, a, r, tmp):
            step(dve.tensor_tensor(tmp, r, r, ALU.mult))
            step(dve.tensor_tensor(tmp, tmp, a, ALU.mult))
            step(dve.tensor_scalar(tmp, tmp, -0.5, 1.5, ALU.mult, ALU.add))
            step(dve.tensor_tensor(out, r, tmp, ALU.mult))

        def normalise(b):
            dve.wait_ge(x_loaded[b % 2], 16 * (b // 2 + 1))
            for i in range(YT):
                step(dve.bn_stats(stats[:, i, :], xin[:, b % 2, i, :]))
            for i in range(YT):
                step(dve.bn_aggr(mv[:, i, :], stats[:, i, :]))
            step(dve.tensor_scalar(rs[:, 2, :], mv[:, :, 1], EPS, None, ALU.add))
            dve.reciprocal(rs[:, 0, :], rs[:, 2, :]).then_inc(var_inv, 1)
            dve.wait_ge(var_root, b + 1)
            newton(rs[:, 3, :], rs[:, 2, :], rs[:, 1, :], rs[:, 0, :])
            if b:
                dve.wait_ge(xt_made, b)
            for i in range(YT):
                last = dve.tensor_scalar(xn[:, i, :], xin[:, b % 2, i, :], mv[:, i, 0:1], rs[:, 3, i:i + 1],
                                         ALU.subtract, ALU.mult)
            last.then_inc(xn_ready, 1)

        def xt_low_part(b):
            dve.wait_ge(xt_high, b + 1)
            dve.tensor_tensor(xtl[:, b % 2, :], ps_x[:, b % 2, :], xtr[:, b % 2, :].bitcast(F32),
                              ALU.subtract).then_inc(xt_low, 1)

        def y_low_part(b):
            dve.wait_ge(y_high, b + 1)
            rows = slice(b * YT, (b + 1) * YT)
            dve.tensor_tensor(zl[:, rows, :].rearrange("p t c -> p (t c)"), ps_y[:, b % 2, :],
                              zr[:, rows, :].rearrange("p t c -> p (t c)").bitcast(F32),
                              ALU.subtract).then_inc(y_low, 1)

        def sum_block(b):
            dve.wait_ge(raw_loaded[b.s], 16 * (b.n // RING + 1))
            out = sum_v[:, b.strip, :]
            src = raw[:, b.s, 0:2, :].rearrange("p s i -> p (s i)")
            if b.n_deg:
                dve.wait_ge(summed_v, b.n_deg)
            if b.jp == b.t and b.s % 2 == 0:
                if b.t:
                    dve.wait_ge(deg_made, b.t)
                dve.tensor_copy(out, src).then_inc(summed_v, 1)
            else:
                dve.tensor_tensor(out, out, src, ALU.add).then_inc(summed_v, 1)

        pending = []
        strips = [0]

        def add_strip():
            b = pending.pop(0)
            dve.wait_ge(block_done, b.n_prod + 1)
            if strips[0]:
                dve.wait_ge(acc_added, strips[0])
            strips[0] += 1
            out = acc[:, b.i * SUB:(b.i + 1) * SUB, :]
            if b.kind == BOTH and b.jp == 0:
                dve.tensor_copy(out, ps_prod[:, b.strip, :, :]).then_inc(acc_added, 1)
            else:
                dve.tensor_tensor(out, ps_prod[:, b.strip, :, :], out, ALU.add).then_inc(acc_added, 1)

        def a_low_part(b):
            dve.wait_ge(a_high, b.n_prod + 1)
            k = b.n_prod % 2
            dve.tensor_tensor(al[:, k, :, :], raw[:, b.s, :, :], ar[:, k, :, :].bitcast(F32),
                              ALU.subtract).then_inc(a_low, 1)
            if pending and pending[0].n_prod + 2 <= b.n_prod:
                add_strip()
            if b.s % 2 == 1:
                pending.append(b)

        dve.wait_ge(w_high, 1)
        dve.tensor_tensor(wl[:, :, :], w_raw[:, :, :], wr[:, :, :].bitcast(F32), ALU.subtract).then_inc(w_low, 1)
        first = list(steps[0][0])
        for b in range(NY + 2):
            if b < NY:
                normalise(b)
            if first:
                sum_block(first.pop(0))
            if 1 <= b <= NY:
                xt_low_part(b - 1)
            if b >= 2:
                y_low_part(b - 2)
        for t, (before, after) in enumerate(steps):
            rows = slice(t * PT, (t + 1) * PT)
            if t:
                for b in before:
                    if b.sums:
                        sum_block(b)
                    if b.multiplies:
                        a_low_part(b)
            step(dve.tensor_tensor(z[:, :, :], zr[:, rows, :].bitcast(F32), zl[:, rows, :].bitcast(F32), ALU.add))
            dve.wait_ge(deg_made, t + 1)
            step(dve.tensor_scalar(dg[:, 0, :], ps_x[:, 0, 0:PT], 1.0, None, ALU.add))
            dve.reciprocal(dg[:, 1, :], dg[:, 0, :]).then_inc(deg_inv, 1)
            dve.wait_ge(deg_root, t + 1)
            newton(dinv[:, rows], dg[:, 0, :], dg[:, 2, :], dg[:, 3, :])
            for i in range(PT):
                last = dve.tensor_scalar(z[:, i, :], z[:, i, :], dinv[:, t * PT + i:t * PT + i + 1], None, ALU.mult)
            last.then_inc(z_scaled, 1)
            dve.wait_ge(z_high, t + 1)
            dve.tensor_tensor(zl[:, rows, :], z[:, :, :], zr[:, rows, :].bitcast(F32), ALU.subtract).then_inc(z_low, 1)
            while pending:
                add_strip()
            if strips[0]:
                dve.wait_ge(acc_added, strips[0])
            if t:
                step(dve.tensor_tensor(acc[:, rows, :], acc[:, rows, :], z[:, :, :], ALU.add))
            else:
                step(dve.tensor_copy(acc[:, rows, :], z[:, :, :]))
            for b in after:
                a_low_part(b)
        while pending:
            add_strip()

    @block.tensor
    def _(pe):
        def transposes(b):
            pe.wait_ge(xn_ready, b + 1)
            if b >= 2:
                pe.wait_ge(xt_low, b - 1)
            for i in range(YT):
                for k in range(KC):
                    at_ = (i * KC + k) * P
                    last = pe.transpose(ps_x[:, b % 2, at_:at_ + P], xn[:, i, k * P:(k + 1) * P], ident)
            last.then_inc(xt_made, 1)

        def y_tiles(b):
            pe.wait_ge(xt_low, b + 1)
            if b >= 2:
                pe.wait_ge(y_low, b - 1)
            for i in range(YT):
                for k in range(KC):
                    at_ = (i * KC + k) * P
                    hi, lo = (v[:, b % 2, at_:at_ + P] for v in (xtr, xtl))
                    for q, (lhs, rhs) in enumerate(((hi, wr), (hi, wl), (lo, wr))):
                        last = pe.matmul(ps_y[:, b % 2, i * C:(i + 1) * C], lhs, rhs[:, k, :],
                                         start=(i == 0 and k == 0 and q == 0), stop=(k == KC - 1 and q == 2),
                                         skip_group_check=True)
            last.then_inc(y_made, 1)

        def product_group(first, added, j_tile):
            for s in range(4):
                strip, half = s // 2, s % 2
                pe.wait_ge(a_low, first + (s + 1))
                if half == 0:
                    if added is not None:
                        pe.wait_ge(acc_added, added + strip)
                for i in range(SUB):
                    for sub in range(SUB):
                        hi, lo = (v[:, s % 2, sub, i * P:(i + 1) * P] for v in (ar, al))
                        tile = j_tile + (half * SUB + sub)
                        mh, ml = (v[:, bass.ds(tile, 1), :].rearrange("p t c -> p (t c)") for v in (zr, zl))
                        for q, (lhs, rhs) in enumerate(((hi, mh), (hi, ml), (lo, mh))):
                            last = pe.matmul(ps_prod[:, strip, i, :], lhs, rhs,
                                             start=(half == 0 and i % 2 == 0 and sub == 0 and q == 0),
                                             stop=(half == 1 and sub == SUB - 1 and q == 2),
                                             skip_group_check=True)
                last.then_inc(block_done, 1)

        def degrees(t):
            n = sum(b.sums for b in every if b.t <= t)
            pe.wait_ge(summed_v, n)
            pe.wait_ge(summed_p, n)
            for i in range(PT):
                strip, at_ = i // SUB, i % SUB * P
                parts = [v[:, strip, h * BW + at_:h * BW + at_ + P] for v in (sum_v, sum_p) for h in range(2)]
                for q, part in enumerate(parts):
                    last = pe.matmul(ps_x[:, 0, i:i + 1], part, ones[:, :], start=(i == 0 and q == 0),
                                     stop=(q == 3), skip_group_check=True)
            last.then_inc(deg_made, 1)

        pe.wait_ge(w_low, 1)
        pe.wait_ge(ones_set, 1)
        pe.wait_ge(const_loaded, 16)
        for b in range(NY + 1):
            if b < NY:
                transposes(b)
            if b:
                y_tiles(b - 1)
        pe.wait_ge(y_low, NY)
        for t, (before, after) in enumerate(steps):
            lower = [b for b in before if b.multiplies]
            if lower:
                base = lower[0].n_prod
                with pe.Fori(0, t) as g:
                    product_group(g * 4 + base, g * 2 + (base // 2 - 1), g * PT)
            degrees(t)
            pe.wait_ge(z_low, t + 1)
            base = after[0].n_prod
            if t == 0:
                product_group(base, None, 0)
            else:
                with pe.Fori(0, t + 1) as g:
                    product_group(g * 4 + base, g * 2 + (base // 2 - 1), t * PT)


def between(nc, ctx, x, gate_w, gate_b, w1, w2, rows, consts, at, acc, dinv, wts, ids, dst, tile_expert, w1r, w1l,
            w2r, w2l):

    def sb(name, shape, dt=F32):
        return ctx.enter_context(nc.sbuf_tensor(name, shape, dt))

    def ps(name, shape):
        return ctx.enter_context(nc.psum_tensor(name, shape, F32))

    def sem(name):
        return ctx.enter_context(nc.semaphore(name))

    xe = sb("xe", [P, 2, YT, C])
    ee = sb("ee", [P, 2, YT, C])
    xh = sb("xh", [P, 2, YT, C])
    xht = ee
    stage = sb("stage", [P, 2, KC * F])
    st2 = sb("st2", [P, YT, 6])
    mv2 = sb("mv2", [P, NT, 2])
    rs2 = sb("rs2", [P, 5, NT])
    gw = sb("gw", [P, KC, E])
    gb = sb("gb", [P, 1, E])

    ps_t = ps("ps_t", [P, 2, BW])
    ps_gate = ps("ps_gate", [P, NT, E])
    ps_cnt = ps("ps_cnt", [P, NT, E])
    ps_tot = ps("ps_tot", [P, NT, E])
    ps_ids = ps("ps_ids", [P, 2, SLOTS])

    gate_loaded = sem("gate_loaded")
    xe_loaded = [sem(f"xe_loaded{i}") for i in range(2)]
    g_ready = sem("g_ready")
    e_ready = sem("e_ready")
    x2_ready = sem("x2_ready")
    r_inv = sem("r_inv")
    r_root = sem("r_root")
    xh_ready = sem("xh_ready")
    xh_made = sem("xh_made")
    xht_ready = sem("xht_ready")
    logit_done = sem("logit_done")
    xh_stored = [sem(f"xh_stored{i}") for i in range(2)]
    v_chain = sem("v_chain2")
    stage_loaded = [sem(f"stage_loaded{i}") for i in range(2)]
    w_hi = sem("w_hi")
    w_lo = sem("w_lo")
    diff_ready = sem("diff_ready")
    exp_ready = sem("exp_ready")
    mask_ready = sem("mask_ready")
    counts_ready = sem("counts_ready")
    hot_ready = sem("hot_ready")
    hot_used = sem("hot_used")
    ids_made = sem("ids_made")

    x_v = x.rearrange("(b t p) c -> b p t c", t=YT, p=P)
    rows_v = rows.rearrange("(b t p) c -> b p t c", t=YT, p=P)

    lg = sb("lg", [P, NT, E])
    l2 = sb("l2", [P, NT, E])
    cand = sb("cand", [P, NT, E])
    hot1 = sb("hot1", [P, NT, E])
    hot2 = sb("hot2", [P, NT, E])
    mask = sb("mask", [P, NT, E])
    col = sb("col", [P, 8, NT])
    tot = sb("tot", [P, E, NT])
    keep = sb("keep", [P, E, NT])
    incl = sb("incl", [P, E, NT])
    ex = sb("ex", [P, 6, E])
    ti = sb("ti", [P, SLOTS, E])
    tf = sb("tf", [P, SLOTS])
    pos = sb("pos", [P, CW])
    pos_i = sb("pos_i", [P, 2, CW], I32)
    pos_f = sb("pos_f", [P, 2, CW])
    hot_r = sb("hot_r", [P, 4, P], BF16)
    hot_q = sb("hot_q", [P, 4, 2, SLOTS], BF16)
    ones = sb("ones2", [P, P])
    v = sb("v", [P, SLOTS])
    pad = sb("pad", [P, SLOTS])
    ones2_set = sem("ones2_set")

    def K(name):
        return consts[:, at[name]]

    def chunks():
        for e in range(E):
            yield w1[e].rearrange("(k p) f -> p k f", p=P), w1r[:, e], w1l[:, e]
        for e in range(E):
            yield w2[e].rearrange("(k p) c -> p k c", p=P), w2r[:, e], w2l[:, e]

    block = ctx.enter_context(nc.Block())

    @block.sync
    def _(sp):
        sp.dma_start(gw[:, :, :], gate_w.rearrange("(k p) e -> p k e", p=P)).then_inc(gate_loaded, 16)
        sp.dma_start(gb[:, 0, :], gate_b.partition_broadcast(P)).then_inc(gate_loaded, 16)

        def load(b, k):
            if not isinstance(b, int) or b >= 2:
                sp.wait_ge(x2_ready, b - 1)
            src = x_v[b] if isinstance(b, int) else x_v[bass.ds(b, 1)].rearrange("b p t c -> p (b t) c")
            sp.dma_start(xe[:, k, :, :], src).then_inc(xe_loaded[k], 16)

        in_pairs(sp, NY, load)

        def store(b, k):
            sp.wait_ge(xh_ready, b + 1)
            to = rows_v[b] if isinstance(b, int) else rows_v[bass.ds(b, 1)].rearrange("b p t c -> p (b t) c")
            sp.dma_start(to, xh[:, k, :, :]).then_inc(xh_stored[k], 16)

        in_pairs(sp, NY, store)
        for k in range(2):
            sp.wait_ge(xh_stored[k], 16 * (NY // 2))

    @block.gpsimd
    def _(pool):
        pool.memset(ones[:, :], 1.0).then_inc(ones2_set, 1)
        pool.memset(keep[:, :, :], 1.0).then_inc(ones2_set, 1)
        pool.wait_ge(ones2_set, 2)
        pool.memset(keep[:, :, 0:1], 0.0).then_inc(ones2_set, 1)
        for n, (src, hi, lo) in enumerate(chunks()):
            def load(m, s):
                pool.dma_start(stage[:, m % 2, :].rearrange("p (k f) -> p k f", k=s.shape[1]), s
                               ).then_inc(stage_loaded[m % 2], 16)
            if n == 0:
                todo = [c[0] for c in chunks()]
                load(0, todo[0])
                load(1, todo[1])
            pool.wait_ge(w_hi, n + 1)
            pool.tensor_tensor(lo.rearrange("p k f -> p (k f)"), stage[:, n % 2, :],
                               hi.rearrange("p k f -> p (k f)").bitcast(F32), ALU.subtract).then_inc(w_lo, 1)
            if n + 2 < 2 * E:
                pool.wait_ge(w_lo, n + 1)
                load(n + 2, todo[n + 2])

    @block.scalar
    def _(act):
        def weights(n):
            hi = list(chunks())[n][1]
            act.wait_ge(stage_loaded[n % 2], 16 * (n // 2 + 1))
            act.activation(hi.rearrange("p k f -> p (k f)"), stage[:, n % 2, :], ACT.Copy).then_inc(w_hi, 1)

        def exps(b, k):
            act.wait_ge(g_ready, b + 1)
            if not isinstance(b, int) or b >= 2:
                act.wait_ge(x2_ready, b - 1)
            act.activation(ee[:, k, :, :], acc[:, bass.ds(b * YT, YT), :], ACT.Exp).then_inc(e_ready, 1)

        in_pairs(act, NY, exps)
        act.wait_ge(r_inv, 1)
        act.activation(rs2[:, 1, :], rs2[:, 0, :], ACT.Sqrt).then_inc(r_root, 1)

        def turned(b, k):
            act.wait_ge(xh_made, b + 1)
            if not isinstance(b, int) or b >= 2:
                act.wait_ge(logit_done, b - 1)
            act.activation(xht[:, k, :, :].rearrange("p t c -> p (t c)"), ps_t[:, k, :], ACT.Copy
                           ).then_inc(xht_ready, 1)

        in_pairs(act, NY, turned)
        act.wait_ge(diff_ready, 1)
        act.activation(col[:, 3, :], col[:, 2, :], ACT.Exp).then_inc(exp_ready, 1)
        for n in range(2 * E):
            weights(n)

    @block.vector
    def _(dve):
        ch = Chain(dve, v_chain)
        step = ch.step

        def g(b):
            for i in range(YT):
                row = acc[:, bass.ds(b * YT + i, 1), :].rearrange("p t c -> p (t c)")
                last = dve.tensor_scalar(row, row, dinv[:, bass.ds(b * YT + i, 1)], None, ALU.mult)
            last.then_inc(g_ready, 1)

        def x2(b, k):
            row = acc[:, bass.ds(b * YT, YT), :].rearrange("p t c -> p (t c)")
            dve.wait_ge(xe_loaded[k], (16 + b // 2 * 16) if isinstance(b, int) else b * 8 + (16 - 8 * k))
            dve.wait_ge(e_ready, b + 1)
            step(dve.scalar_tensor_tensor(row, row, 0.0, xe[:, k, :, :].rearrange("p t c -> p (t c)"),
                                          ALU.max, ALU.add))
            dve.scalar_tensor_tensor(row, ee[:, k, :, :].rearrange("p t c -> p (t c)"), 1.0, row,
                                     ALU.min, ALU.add).then_inc(x2_ready, 1)
            if not isinstance(b, int) or b < NY - 1:
                pass
            dve.wait_ge(x2_ready, b + 1)
            for i in range(YT):
                step(dve.bn_stats(st2[:, i, :], acc[:, bass.ds(b * YT + i, 1), :].rearrange("p t c -> p (t c)")))
            for i in range(YT):
                step(dve.bn_aggr(mv2[:, bass.ds(b * YT + i, 1), :].rearrange("p t c -> p (t c)"), st2[:, i, :]))

        def both(b, k):
            g(b)
            x2(b, k)

        for b in range(NY):
            both(b, b % 2)
        a, root, rstd, tmp = rs2[:, 2, :], rs2[:, 1, :], rs2[:, 3, :], rs2[:, 4, :]
        step(dve.tensor_scalar(a, mv2[:, :, 1], EPS, None, ALU.add))
        dve.reciprocal(rs2[:, 0, :], a).then_inc(r_inv, 1)
        dve.wait_ge(r_root, 1)
        step(dve.tensor_tensor(tmp, root, root, ALU.mult))
        step(dve.tensor_tensor(tmp, tmp, a, ALU.mult))
        step(dve.tensor_scalar(tmp, tmp, -0.5, 1.5, ALU.mult, ALU.add))
        step(dve.tensor_tensor(rstd, root, tmp, ALU.mult))

        def norm(b, k):
            if not isinstance(b, int) or b >= 2:
                dve.wait_ge(xh_stored[k], (b // 2 * 16) if isinstance(b, int) else b * 8 - 8 * k)
                dve.wait_ge(xh_made, b - 1)
            for i in range(YT):
                t = b * YT + i
                last = dve.tensor_scalar(xh[:, k, i, :], acc[:, bass.ds(t, 1), :].rearrange("p t c -> p (t c)"),
                                         mv2[:, bass.ds(t, 1), 0], rs2[:, 3, bass.ds(t, 1)],
                                         ALU.subtract, ALU.mult)
            last.then_inc(xh_ready, 1)

        in_pairs(dve, NY, norm)

        def over_e(ap):
            return ap.unsqueeze(2).broadcast_to([P, NT, E])

        def over_t(ap):
            return ap.unsqueeze(1).broadcast_to([P, NT, E])

        dve.wait_ge(logit_done, NY)
        dve.wait_ge(gate_loaded, 32)
        step(dve.tensor_tensor(lg[:, :, :], ps_gate[:, :, :], gb[:, :, :].broadcast_to([P, NT, E]), ALU.add))
        idx = over_t(K("expert"))

        def pick(src, top, hot):
            step(dve.tensor_reduce(top, src, AX.X, ALU.max))
            step(dve.tensor_tensor(cand[:, :, :], src, over_e(top), ALU.is_equal))
            step(dve.scalar_tensor_tensor(cand[:, :, :], cand[:, :, :], -float(E), idx, ALU.mult, ALU.add))
            step(dve.tensor_reduce(col[:, 7, :], cand[:, :, :], AX.X, ALU.min))
            step(dve.tensor_tensor(hot, cand[:, :, :], over_e(col[:, 7, :]), ALU.is_equal))

        pick(lg[:, :, :], col[:, 0, :], hot1[:, :, :])
        step(dve.scalar_tensor_tensor(l2[:, :, :], hot1[:, :, :], -FAR, lg[:, :, :], ALU.mult, ALU.add))
        pick(l2[:, :, :], col[:, 1, :], hot2[:, :, :])
        dve.tensor_tensor(col[:, 2, :], col[:, 1, :], col[:, 0, :], ALU.subtract).then_inc(diff_ready, 1)
        dve.tensor_tensor(mask[:, :, :], hot1[:, :, :], hot2[:, :, :], ALU.add).then_inc(mask_ready, 1)
        dve.wait_ge(exp_ready, 1)
        step(dve.tensor_scalar(col[:, 4, :], col[:, 3, :], 1.0, None, ALU.add))
        step(dve.reciprocal(wts[:, 0, :], col[:, 4, :]))
        step(dve.tensor_tensor(wts[:, 1, :], wts[:, 0, :], col[:, 3, :], ALU.mult))
        dve.wait_ge(counts_ready, 1)
        dve.wait_ge(ones2_set, 3)
        step(dve.tensor_copy(tot[:, :, :], ps_tot[:, :, :].rearrange("p t e -> p e t")))
        step(dve.tensor_tensor_scan(incl[:, :, :].rearrange("p e t -> p (e t)"),
                                    keep[:, :, :].rearrange("p e t -> p (e t)"),
                                    tot[:, :, :].rearrange("p e t -> p (e t)"), 0.0, ALU.mult, ALU.add))
        rows_e = incl[:, :, NT - 1:NT].broadcast_to([P, E, NT])
        full = cand[:, :, :].rearrange("p t e -> p (t e)").rearrange("p (e t) -> p e t", e=E)
        step(dve.tensor_tensor(full, rows_e, K("step").unsqueeze(1).broadcast_to([P, E, NT]), ALU.is_gt))
        step(dve.tensor_reduce(ex[:, 0, :], full, AX.X, ALU.add))
        step(dve.tensor_tensor_scan(ex[:, 1, :], ones[:, 0:E], ex[:, 0, :], 0.0, ALU.mult, ALU.add))
        step(dve.tensor_tensor(ex[:, 2, :], ex[:, 1, :], ex[:, 0, :], ALU.subtract))
        step(dve.tensor_scalar(ex[:, 3, :], ex[:, 2, :], float(P), None, ALU.mult))
        step(dve.tensor_tensor(incl[:, :, :], incl[:, :, :], tot[:, :, :], ALU.subtract))
        step(dve.tensor_tensor(incl[:, :, :], incl[:, :, :], ex[:, 3, :].unsqueeze(2).broadcast_to([P, E, NT]),
                               ALU.add))
        step(dve.tensor_tensor(l2[:, :, :], ps_cnt[:, :, :], incl[:, :, :].rearrange("p e t -> p t e"), ALU.add))
        for k, hot in enumerate((hot1, hot2)):
            step(dve.tensor_tensor(cand[:, :, :], hot[:, :, :], l2[:, :, :], ALU.mult))
            step(dve.tensor_reduce(pos[:, k * NT:(k + 1) * NT], cand[:, :, :], AX.X, ALU.add))
        step(dve.tensor_copy(pos_i[:, 0, :], pos[:, :]))
        step(dve.tensor_scalar(pos_i[:, 1, :], pos_i[:, 0, :], P - 1, None, ALU.bitwise_and))
        step(dve.tensor_copy(pos_f[:, 1, :], pos_i[:, 1, :]))
        step(dve.tensor_tensor(pos_f[:, 0, :], pos[:, :], pos_f[:, 1, :], ALU.subtract))
        step(dve.tensor_scalar(pos_f[:, 0, :], pos_f[:, 0, :], 1.0 / P, None, ALU.mult))

        def hots(c, k):
            if not isinstance(c, int) or c >= 4:
                dve.wait_ge(hot_used, c - 3)
            q, r = pos_f[:, 0, bass.ds(c, 1)], pos_f[:, 1, bass.ds(c, 1)]
            dve.tensor_scalar(hot_r[:, k, :], K("lane"), r, None, ALU.is_equal)
            dve.tensor_scalar(hot_q[:, k, 0, :], K("tile"), q, consts[:, bass.ds(c + at["column"].start, 1)],
                              ALU.is_equal, ALU.mult)
            dve.tensor_scalar(hot_q[:, k, 1, :], K("tile"), q, K("row"),
                              ALU.is_equal, ALU.mult).then_inc(hot_ready, 1)

        for c in range(4):
            hots(c, c)
        with dve.Fori(1, CW // 4) as i:
            for c in range(4):
                hots(i * 4 + c, c)
        step(dve.tensor_tensor(ti[:, :, :], ex[:, 1:2, :].broadcast_to([P, SLOTS, E]),
                               K("tile").unsqueeze(2).broadcast_to([P, SLOTS, E]), ALU.is_le))
        step(dve.tensor_reduce(tf[:, :], ti[:, :, :], AX.X, ALU.add))
        step(dve.tensor_scalar(tile_expert[:, :], tf[:, :], float(E - 1), None, ALU.min))
        dve.wait_ge(ids_made, 1)
        step(dve.tensor_scalar(v[:, :], ps_ids[:, 0, :], float(P), -float(P), ALU.mult, ALU.add))
        step(dve.tensor_tensor(v[:, :], v[:, :], ps_ids[:, 1, :], ALU.add))
        step(dve.tensor_scalar(pad[:, :], v[:, :], 0.0, None, ALU.is_lt))
        step(dve.tensor_scalar(tf[:, :], K("row").broadcast_to([P, SLOTS]), float(PAD_ROW + P), None, ALU.add))
        step(dve.tensor_tensor(tf[:, :], tf[:, :], pad[:, :], ALU.mult))
        step(dve.tensor_tensor(dst[:, :], tf[:, :], v[:, :], ALU.add))
        step(dve.tensor_scalar(tf[:, :], v[:, :], float(N), -float(N), ALU.is_ge, ALU.mult))
        step(dve.tensor_scalar(v[:, :], v[:, :], 0.0, None, ALU.max))
        step(dve.tensor_tensor(ids[:, :], tf[:, :], v[:, :], ALU.add))

    @block.tensor
    def _(pe):
        def turn(b, k):
            pe.wait_ge(xh_ready, b + 1)
            if not isinstance(b, int) or b >= 2:
                pe.wait_ge(xht_ready, b - 1)
            for i in range(YT):
                for c in range(KC):
                    a = (i * KC + c) * P
                    last = pe.transpose(ps_t[:, k, a:a + P], xh[:, k, i, c * P:(c + 1) * P], K("ident"))
            last.then_inc(xh_made, 1)
            logits(b, k)

        def logits(b, k):
            pe.wait_ge(xht_ready, b + 1)
            for i in range(YT):
                for c in range(KC):
                    a = (i * KC + c) * P
                    src = xht[:, k, :, :].rearrange("p t c -> p (t c)")[:, a:a + P]
                    out = ps_gate[:, bass.ds(b * YT + i, 1), :].rearrange("p t e -> p (t e)")
                    last = pe.matmul(out, src, gw[:, c, :], start=(c == 0), stop=(c == KC - 1),
                                     skip_group_check=True)
            last.then_inc(logit_done, 1)

        pe.wait_ge(gate_loaded, 32)
        in_pairs(pe, NY, turn)
        pe.wait_ge(mask_ready, 1)
        pe.wait_ge(ones2_set, 1)
        flat = mask[:, :, :].rearrange("p t e -> p (t e)")
        pe.matmul(ps_cnt[:, :, :].rearrange("p t e -> p (t e)"), K("before"), flat, start=True, stop=True)
        pe.matmul(ps_tot[:, :, :].rearrange("p t e -> p (t e)"), ones[:, :], flat, start=True,
                  stop=True).then_inc(counts_ready, 1)

        def place(c, k):
            pe.wait_ge(hot_ready, c + 1)
            return pe.matmul(ps_ids[:, :, :].rearrange("p h q -> p (h q)"), hot_r[:, k, :],
                             hot_q[:, k, :, :].rearrange("p h q -> p (h q)"),
                             start=(isinstance(c, int) and c == 0), stop=False, skip_group_check=True
                             ).then_inc(hot_used, 1)

        for c in range(4):
            place(c, c)
        with pe.Fori(1, CW // 4) as i:
            for c in range(4):
                place(i * 4 + c, c)
        pe.wait_ge(hot_used, CW)
        pe.nop().then_inc(ids_made, 1)


def experts(nc, ctx, b1, b2, rows, parts, consts, at, ids, dst, tile_expert, w1r, w1l, w2r, w2l):

    def sb(name, shape, dt=F32):
        return ctx.enter_context(nc.sbuf_tensor(name, shape, dt))

    def ps(name, shape):
        return ctx.enter_context(nc.psum_tensor(name, shape, F32))

    def sem(name):
        return ctx.enter_context(nc.semaphore(name))

    b1a = sb("b1a", [P, E, F])
    b2a = sb("b2a", [P, E, C])
    xg = sb("xg", [P, 2, C])
    xgr = sb("xgr", [P, C], F32R)
    xgl = sb("xgl", [P, C], F32R)
    h = sb("h", [P, F])
    hr = sb("hr", [P, 2, F], F32R)
    hl = sb("hl", [P, 2, F], F32R)
    yo = sb("yo", [P, 2, C])

    ps_h = ps("ps_h", [P, 2, F])
    ps_xt = ps("ps_xt", [P, 1, BW])
    ps_ht = ps("ps_ht", [P, 2, F])
    ps_o = ps("ps_o", [P, 2, BW])

    b_loaded = sem("b_loaded")
    xg_loaded = [sem(f"xg_loaded{i}") for i in range(2)]
    yo_stored = [sem(f"yo_stored{i}") for i in range(2)]
    xg_turned = sem("xg_turned")
    xg_high = sem("xg_high")
    xg_low = sem("xg_low")
    h_made = sem("h_made")
    h_ready = sem("h_ready")
    h_turned = sem("h_turned")
    h_high = sem("h_high")
    h_low = sem("h_low")
    o_made = sem("o_made")
    o_ready = sem("o_ready")

    block = ctx.enter_context(nc.Block())

    def is_int(q):
        return isinstance(q, int)

    def stages(eng, stage):
        for q in range(-1, 3):
            stage(q, q % 2)
        with eng.Fori(1, SLOTS // 2 - 1) as i:
            stage(i * 2 + 1, 1)
            stage(i * 2 + 2, 0)
        for q in range(SLOTS - 1, SLOTS + 1):
            stage(q, q % 2)

    @block.sync
    def _(sp):
        sp.dma_start(b1a[:, :, :], b1.rearrange("e f -> (e f)").partition_broadcast(P)).then_inc(b_loaded, 16)
        sp.dma_start(b2a[:, :, :], b2.rearrange("e f -> (e f)").partition_broadcast(P)).then_inc(b_loaded, 16)

    @block.gpsimd
    def _(pool):
        def gather(q):
            if q >= 2:
                pool.wait_ge(xg_turned, q - 1)
            pool.indirect_dma_start(xg[:, q % 2, :], None, rows,
                                    bass.IndirectOffsetOnAxis(ap=ids[:, q:q + 1].bitcast(U32), axis=0)
                                    ).then_inc(xg_loaded[q % 2], 16)

        def scatter(q):
            pool.wait_ge(o_ready, q + 1)
            if q >= 1:
                pool.wait_ge(yo_stored[1 - q % 2], 16 * ((q + 1) // 2))
            pool.indirect_dma_start(parts,
                                    bass.IndirectOffsetOnAxis(ap=dst[:, q:q + 1].bitcast(U32), axis=0),
                                    yo[:, q % 2, :], None).then_inc(yo_stored[q % 2], 16)

        for q in range(SLOTS + 2):
            if q < SLOTS:
                gather(q)
            if q >= 2:
                scatter(q - 2)
        for k in range(2):
            pool.wait_ge(yo_stored[k], 8 * SLOTS)

    @block.scalar
    def _(act):
        def stage(q, k):
            if not is_int(q) or q + 1 < SLOTS:
                act.wait_ge(xg_turned, q + 2)
                if not is_int(q) or q >= 0:
                    act.wait_ge(h_made, q + 1)
                act.activation(xgr[:, :], ps_xt[:, 0, 0:C], ACT.Copy).then_inc(xg_high, 1)
            if not is_int(q) or 0 <= q < SLOTS:
                act.wait_ge(h_turned, q + 1)
                if not is_int(q) or q >= 2:
                    act.wait_ge(o_made, q - 1)
                act.activation(hr[:, k, :], ps_ht[:, k, :], ACT.Relu).then_inc(h_high, 1)

        stages(act, stage)

    @block.vector
    def _(dve):
        dve.wait_ge(b_loaded, 32)

        def stage(q, k):
            if not is_int(q) or 0 <= q < SLOTS:
                e = dve.value_load(tile_expert[0:1, bass.ds(q, 1)], min_val=0, max_val=E - 1)
                dve.wait_ge(h_made, q + 1)
                if not is_int(q) or q >= 1:
                    dve.wait_ge(h_turned, q)
                dve.tensor_tensor(h[:, :], ps_h[:, k, :], b1a[:, bass.ds(e, 1), :].rearrange("p e f -> p (e f)"),
                                  ALU.add).then_inc(h_ready, 1)
            if not is_int(q) or q + 1 < SLOTS:
                dve.wait_ge(xg_high, q + 2)
                dve.tensor_tensor(xgl[:, :], ps_xt[:, 0, 0:C], xgr[:, :].bitcast(F32),
                                  ALU.subtract).then_inc(xg_low, 1)
            if not is_int(q) or 0 <= q < SLOTS:
                dve.wait_ge(h_high, q + 1)
                dve.scalar_tensor_tensor(hl[:, k, :], ps_ht[:, k, :], 0.0, hr[:, k, :].bitcast(F32),
                                         ALU.max, ALU.subtract).then_inc(h_low, 1)
            if not is_int(q) or q >= 1:
                e = dve.value_load(tile_expert[0:1, bass.ds(q - 1, 1)], min_val=0, max_val=E - 1)
                dve.wait_ge(o_made, q)
                if not is_int(q) or q >= 3:
                    dve.wait_ge(yo_stored[1 - k], q * 8 - 8 if k else q * 8 - 16)
                dve.tensor_tensor(yo[:, 1 - k, :], ps_o[:, 1 - k, 0:C],
                                  b2a[:, bass.ds(e, 1), :].rearrange("p e f -> p (e f)"),
                                  ALU.add).then_inc(o_ready, 1)

        stages(dve, stage)

    @block.tensor
    def _(pe):
        ident = consts[:, at["ident"]]

        def stage(q, k):
            if not is_int(q) or 0 <= q < SLOTS:
                e = pe.value_load(tile_expert[0:1, bass.ds(q, 1)], min_val=0, max_val=E - 1)
                pe.wait_ge(xg_low, q + 1)
                if not is_int(q) or q >= 2:
                    pe.wait_ge(h_ready, q - 1)
                for c in range(KC):
                    hi, lo = xgr[:, c * P:(c + 1) * P], xgl[:, c * P:(c + 1) * P]
                    mh, ml = (v[:, bass.ds(e, 1), c, :].rearrange("p e f -> p (e f)") for v in (w1r, w1l))
                    for n, (lhs, rhs) in enumerate(((hi, mh), (hi, ml), (lo, mh))):
                        last = pe.matmul(ps_h[:, k, :], lhs, rhs, start=(c == 0 and n == 0),
                                         stop=(c == KC - 1 and n == 2))
                last.then_inc(h_made, 1)
            if not is_int(q) or q + 1 < SLOTS:
                n = q + 1
                pe.wait_ge(xg_loaded[1 - k], n * 8 + 16 - 8 * (1 - k))
                if not is_int(q) or q >= 0:
                    pe.wait_ge(xg_low, n)
                for c in range(KC):
                    last = pe.transpose(ps_xt[:, 0, c * P:(c + 1) * P], xg[:, 1 - k, c * P:(c + 1) * P], ident)
                last.then_inc(xg_turned, 1)
            if not is_int(q) or q >= 1:
                e = pe.value_load(tile_expert[0:1, bass.ds(q - 1, 1)], min_val=0, max_val=E - 1)
                pe.wait_ge(h_low, q)
                if not is_int(q) or q >= 3:
                    pe.wait_ge(o_ready, q - 2)
                for c in range(KF):
                    hi, lo = hr[:, 1 - k, c * P:(c + 1) * P], hl[:, 1 - k, c * P:(c + 1) * P]
                    mh, ml = (v[:, bass.ds(e, 1), c, :].rearrange("p e f -> p (e f)") for v in (w2r, w2l))
                    for n, (lhs, rhs) in enumerate(((hi, mh), (hi, ml), (lo, mh))):
                        last = pe.matmul(ps_o[:, 1 - k, 0:C], lhs, rhs, start=(c == 0 and n == 0),
                                         stop=(c == KF - 1 and n == 2))
                last.then_inc(o_made, 1)
            if not is_int(q) or 0 <= q < SLOTS:
                pe.wait_ge(h_ready, q + 1)
                if not is_int(q) or q >= 2:
                    pe.wait_ge(h_low, q - 1)
                for c in range(KF):
                    last = pe.transpose(ps_ht[:, k, c * P:(c + 1) * P], h[:, c * P:(c + 1) * P], ident)
                last.then_inc(h_turned, 1)

        stages(pe, stage)


def combine(nc, ctx, parts, out, acc, wts):

    def sem(name):
        return ctx.enter_context(nc.semaphore(name))

    CT = 4
    y = ctx.enter_context(nc.sbuf_tensor("y", [P, 2, 2, CT, C], F32))
    o = ctx.enter_context(nc.sbuf_tensor("o", [P, 2, CT, C], F32))
    y_loaded = [sem(f"y_loaded{i}") for i in range(2)]
    o_stored = [sem(f"o_stored{i}") for i in range(2)]
    second = sem("second")
    first_added = sem("first_added")
    out_ready = sem("out_ready")
    parts_v = parts[0:2 * N, :].rearrange("(k b t p) c -> k b p t c", k=2, t=CT, p=P)
    out_v = out.rearrange("(b t p) c -> b p t c", t=CT, p=P)
    NBATCH = NT // CT

    def store(act, b):
        act.wait_ge(out_ready, b + 1)
        act.dma_start(out_v[b], o[:, b % 2, :, :]).then_inc(o_stored[b % 2], 16)

    block = ctx.enter_context(nc.Block())

    @block.sync
    def _(sp):
        for b in range(NBATCH):
            if b >= 2:
                sp.wait_ge(out_ready, b - 1)
            for k in range(2):
                sp.dma_start(y[:, b % 2, k, :, :], parts_v[k, b]).then_inc(y_loaded[b % 2], 16)

    @block.scalar
    def _(act):
        for b in range(NBATCH):
            act.wait_ge(y_loaded[b % 2], 32 * (b // 2 + 1))
            if b >= 2:
                act.wait_ge(o_stored[b % 2], 16 * (b // 2))
            for i in range(CT):
                last = act.activation(o[:, b % 2, i, :], y[:, b % 2, 1, i, :], ACT.Copy, bias=-1.0,
                                      scale=wts[:, 1, b * CT + i:b * CT + i + 1])
            last.then_inc(second, 1)
            if b:
                store(act, b - 1)
        store(act, NBATCH - 1)
        for k in range(2):
            act.wait_ge(o_stored[k], 16 * (NBATCH // 2))

    @block.vector
    def _(dve):
        for b in range(NBATCH):
            dve.wait_ge(y_loaded[b % 2], 32 * (b // 2 + 1))
            for i in range(CT):
                t = b * CT + i
                last = dve.scalar_tensor_tensor(acc[:, t, :], y[:, b % 2, 0, i, :], wts[:, 0, t:t + 1],
                                                acc[:, t, :], ALU.mult, ALU.add)
            last.then_inc(first_added, 1)
            dve.wait_ge(first_added, b + 1)
            dve.wait_ge(second, b + 1)
            ov = o[:, b % 2, :, :]
            dve.tensor_tensor(ov, ov, acc[:, b * CT:(b + 1) * CT, :], ALU.add).then_inc(out_ready, 1)


def graph_then_experts(nc, x, adj, w, gate_w, gate_b, w1, b1, w2, b2, const, out):
    at, width = const_slices()
    rows = nc.dram_tensor("rows", [N, C], F32, kind="Internal").ap()
    parts = nc.dram_tensor("parts", [2 * N + P, C], F32, kind="Internal").ap()
    with ExitStack() as whole:
        def sb(ctx, name, shape, dt=F32):
            return ctx.enter_context(nc.sbuf_tensor(name, shape, dt))

        consts = sb(whole, "consts", [P, width])
        dinv = sb(whole, "dinv", [P, NT])
        wts = sb(whole, "wts", [P, 2, NT])
        ids = sb(whole, "ids", [P, SLOTS], I32)
        dst = sb(whole, "dst", [P, SLOTS], I32)
        tile_expert = sb(whole, "tile_expert", [P, SLOTS], I32)
        acc = sb(whole, "acc", [P, NT, C])
        with ExitStack() as ctx:
            graph_layer(nc, ctx, x, adj, w, const, consts, at, acc, dinv)
        with ExitStack() as weights:
            w1r, w1l = (sb(weights, n, [P, E, KC, F], F32R) for n in ("w1r", "w1l"))
            w2r, w2l = (sb(weights, n, [P, E, KF, C], F32R) for n in ("w2r", "w2l"))
            with ExitStack() as ctx:
                between(nc, ctx, x, gate_w, gate_b, w1, w2, rows, consts, at, acc, dinv, wts, ids, dst,
                        tile_expert, w1r, w1l, w2r, w2l)
            with ExitStack() as ctx:
                experts(nc, ctx, b1, b2, rows, parts, consts, at, ids, dst, tile_expert, w1r, w1l, w2r, w2l)
        with ExitStack() as ctx:
            combine(nc, ctx, parts, out, acc, wts)


def constants():
    import numpy as np
    lane = np.arange(P)
    table = dict(ident=np.eye(P), before=lane[:, None] < lane[None, :], lane=lane, tile=np.arange(SLOTS),
                 expert=np.arange(E), step=P * np.arange(NT), column=1 + np.arange(CW), row=lane[:, None])
    parts = [np.broadcast_to(table[name], (P, width)) for name, width in WIDTHS.items()]
    return np.ascontiguousarray(np.concatenate(parts, 1).astype(np.float32))


def kernel(**inputs):
    import numpy as np
    import concourse.bacc as bacc
    from concourse.bass_utils import run_bass_kernel_spmd as run

    nc = bacc.Bacc("TRN2", target_bir_lowering=False, num_devices=1)
    a = {name: np.ascontiguousarray(v) for name, v in inputs.items()}
    blocks = a["adj"].T.reshape(NB, SUB, P, NB, BW).transpose(0, 3, 2, 1, 4)
    arrays = {
        "x_in": a["x"], "adj_in": np.ascontiguousarray(blocks), "w_in": a["L0_gnn_w"],
        "gate_w_in": a["L0_ffn_gate_w"], "gate_b_in": a["L0_ffn_gate_b"], "w1_in": a["L0_ffn_w1"],
        "b1_in": a["L0_ffn_b1"], "w2_in": a["L0_ffn_w2"], "b2_in": a["L0_ffn_b2"], "const_in": constants(),
    }
    args = [nc.dram_tensor(name, v.shape, mybir.dt.from_np(v.dtype), kind="ExternalInput").ap()
            for name, v in arrays.items()]
    args.append(nc.dram_tensor("out_0", (N, C), F32, kind="ExternalOutput").ap())
    graph_then_experts(nc, *args)
    r = run(nc, [arrays], core_ids=[0])
    return r.results[0]["out_0"]
```

```python
from contextlib import ExitStack

import concourse.bass as bass
from concourse import mybir

F32 = mybir.dt.float32
F32R = mybir.dt.float32r
BF16 = mybir.dt.bfloat16
I32 = mybir.dt.int32
U32 = mybir.dt.uint32
ALU = mybir.AluOpType
ACT = mybir.ActivationFunctionType
AX = mybir.AxisListType

P = 128
N = 4096
C = 256
KC = C // P
NT = N // P
BW = 512
SUB = BW // P
NB = N // BW
NPAIR = NB // 2
PT = 2 * SUB
RING = 4
YT = 2
NY = NT // YT
EPS = 1e-5

DEG, BOTH, PROD = "deg", "both", "prod"


def plan():
    steps = []
    for t in range(NPAIR):
        before = [(DEG, jp, t) for jp in range(t, NPAIR)] + [(BOTH, jp, t) for jp in range(t)]
        steps.append((before, [(PROD, t, ip) for ip in range(t + 1)]))
    return steps
E = 8
F = 512
KF = F // P
SLOTS = 2 * NT + E - 1
PAD_ROW = 2 * N
FAR = 3.0e38
CW = 2 * NT

WIDTHS = dict(ident=P, before=P, lane=P, tile=SLOTS, expert=E, step=NT, column=CW, row=1)


def const_slices():
    at, out = 0, {}
    for name, width in WIDTHS.items():
        out[name] = slice(at, at + width)
        at += width
    return out, at


class Chain:

    def __init__(self, eng, sem):
        self.eng, self.sem, self.base, self.n = eng, sem, 0, 0

    def step(self, ins):
        self.n += 1
        ins.then_inc(self.sem, 1)
        self.eng.wait_ge(self.sem, self.base + self.n)


class Block:

    def __init__(self, n, kind, t, jp, ip, s, n_deg, n_prod):
        self.n, self.kind, self.t, self.jp, self.ip, self.s = n, kind, t, jp, ip, s
        self.j, self.strip, self.i = 2 * jp + s % 2, s // 2, 2 * ip + s // 2
        self.sums = kind != PROD
        self.multiplies = kind != DEG
        self.n_deg, self.n_prod = n_deg, n_prod


def blocks_of(steps):
    out, n, n_deg, n_prod = [], 0, 0, 0
    for t, parts in enumerate(steps):
        both = []
        for part in parts:
            row = []
            for kind, jp, ip in part:
                for s in range(4):
                    row.append(Block(n, kind, t, jp, ip, s, n_deg, n_prod))
                    n += 1
                    n_deg += kind != PROD
                    n_prod += kind != DEG
            both.append(row)
        out.append(both)
    return out


def graph_layer(nc, ctx, x, adj, w, gate_w, gate_b, const, rows, consts, at_const, acc, lg):
    steps = blocks_of(plan())
    every = [b for step in steps for part in step for b in part]
    at = {b.n: b for b in every}
    last_t = NPAIR - 1

    def sb(name, shape, dt=F32):
        return ctx.enter_context(nc.sbuf_tensor(name, shape, dt))

    def ps(name, shape):
        return ctx.enter_context(nc.psum_tensor(name, shape, F32))

    def sem(name):
        return ctx.enter_context(nc.semaphore(name))

    zr = sb("zr", [P, NT, C], F32R)
    zl = sb("zl", [P, NT, C], F32R)
    z = sb("z", [P, PT, C])
    raw = sb("raw", [P, RING, SUB, BW])
    ar = sb("ar", [P, 2, SUB, BW], F32R)
    al = sb("al", [P, 2, SUB, BW], F32R)
    sum_v = sb("sum_v", [P, 2, 2, BW])
    sum_p = sb("sum_p", [P, 2, 2, BW])
    w_raw = sb("w_raw", [P, KC, C])
    wr = sb("wr", [P, KC, C], F32R)
    wl = sb("wl", [P, KC, C], F32R)
    xtr = sb("xtr", [P, 2, YT * C], F32R)
    xtl = sb("xtl", [P, 2, YT * C], F32R)
    ones = sb("ones", [P, 1])
    stats = sb("stats", [P, PT, 6])
    mv = sb("mv", [P, NT, 2])
    rs = sb("rs", [P, 4, PT])
    dinv = sb("dinv", [P, NT])
    gw = sb("gw", [P, KC, E])
    gb = sb("gb", [P, 1, E])
    flat = "p t c -> p (t c)"
    xe = [z[:, YT * k:YT * (k + 1), :].rearrange(flat) for k in range(2)]
    ee = [z[:, YT * (k + 2):YT * (k + 3), :].rearrange(flat) for k in range(2)]
    xh = [sum_v[:, k // 2, k % 2, :] for k in range(4)]
    xht = [sum_p[:, k // 2, k % 2, :] for k in range(4)]

    ps_prod = ps("ps_prod", [P, 2, SUB, C])
    ps_x = ps("ps_x", [P, 2, BW])
    ps_y = ps("ps_y", [P, 2, BW])
    ps_gate = ps_y[:, 0, 0:NT * E].rearrange("p (t e) -> p t e", e=E)

    const_loaded = sem("const_loaded")
    w_loaded = sem("w_loaded")
    gate_loaded = sem("gate_loaded")
    ident = consts[:, at_const["ident"]]
    x_loaded = [sem(f"x_loaded{i}") for i in range(NPAIR)]
    raw_loaded = [sem(f"raw_loaded{i}") for i in range(RING)]
    ones_set = sem("ones_set")
    w_high = sem("w_high")
    w_low = sem("w_low")
    v_step = sem("v_step")
    var_inv = sem("var_inv")
    var_root = sem("var_root")
    xn_ready = sem("xn_ready")
    xt_made = sem("xt_made")
    xt_high = sem("xt_high")
    xt_low = sem("xt_low")
    y_made = sem("y_made")
    y_high = sem("y_high")
    y_low = sem("y_low")
    summed_v = sem("summed_v")
    summed_p = sem("summed_p")
    folded_p = sem("folded_p")
    folded = sem("folded")
    deg_made = sem("deg_made")
    deg_inv = sem("deg_inv")
    deg_root = sem("deg_root")
    z_scaled = sem("z_scaled")
    z_high = sem("z_high")
    z_low = sem("z_low")
    z_added = sem("z_added")
    a_high = sem("a_high")
    a_low = sem("a_low")
    block_done = sem("block_done")
    acc_added = sem("acc_added")
    xe_loaded = [sem(f"xe_loaded{i}") for i in range(2)]
    g_ready = sem("g_ready")
    e_ready = sem("e_ready")
    relu_made = sem("relu_made")
    relu_added = sem("relu_added")
    x2_ready = sem("x2_ready")
    var2_inv = sem("var2_inv")
    var2_root = sem("var2_root")
    xh_ready = sem("xh_ready")
    xh_turned = sem("xh_turned")
    xht_ready = sem("xht_ready")
    logits_made = sem("logits_made")
    rows_stored = [sem(f"rows_stored{i}") for i in range(4)]
    lg_ready = sem("lg_ready")

    x_pair = x.rearrange("(b t p) c -> b p t c", t=PT, p=P)
    x_v = x.rearrange("(b t p) c -> b p t c", t=YT, p=P)
    rows_v = rows.rearrange("(b t p) c -> b p t c", t=YT, p=P)
    BP = PT // YT

    def n_sums(t):
        return sum(b.sums for b in every if b.t <= t)

    block = ctx.enter_context(nc.Block())

    @block.sync
    def _(sp):
        def load_x(t):
            sp.dma_start(acc[:, t * PT:(t + 1) * PT, :], x_pair[t]).then_inc(x_loaded[t], 16)

        def store_rows(pair):
            for q in range(BP):
                b = pair * BP + q
                sp.wait_ge(xh_ready, b + 1)
                sp.dma_start(rows_v[b], xh[q].rearrange("p (t c) -> p t c", t=YT)).then_inc(rows_stored[q], 16)

        load_x(0)
        sp.dma_start(w_raw[:, :, :], w.rearrange("(k p) c -> p k c", p=P)).then_inc(w_loaded, 16)
        sp.dma_start(consts[:, :], const).then_inc(const_loaded, 16)
        for b in every:
            if b.n >= RING:
                old = at[b.n - RING]
                if old.sums:
                    sp.wait_ge(summed_v, old.n_deg + 1)
                    sp.wait_ge(summed_p, old.n_deg + 1)
                if old.multiplies:
                    sp.wait_ge(a_low, old.n_prod + 1)
            sp.dma_start(raw[:, b.s, :, :], adj[b.j, b.i]).then_inc(raw_loaded[b.s], 16)
            if b.n in (0, 1, 2):
                load_x(b.n + 1)
            if b.n == RING:
                sp.dma_start(gw[:, :, :], gate_w.rearrange("(k p) e -> p k e", p=P)).then_inc(gate_loaded, 16)
                sp.dma_start(gb[:, 0, :], gate_b.partition_broadcast(P)).then_inc(gate_loaded, 16)
            if b.kind == PROD and b.t == last_t and b.ip >= 2 and b.s == 3:
                store_rows(b.ip - 2)
        for pair in range(NPAIR - 2, NPAIR):
            store_rows(pair)
        for q in range(4):
            sp.wait_ge(rows_stored[q], 16 * NPAIR)

    @block.gpsimd
    def _(pool):
        pool.memset(ones[:, :], 1.0).then_inc(ones_set, 1)
        for t in range(NPAIR):
            for b in every:
                if not b.sums or b.t != t:
                    continue
                pool.wait_ge(raw_loaded[b.s], 16 * (b.n // RING + 1))
                out = sum_p[:, b.strip, :, :]
                src = raw[:, b.s, 2:4, :]
                if b.n_deg:
                    pool.wait_ge(summed_p, b.n_deg)
                if b.jp == b.t and b.s % 2 == 0:
                    if b.t:
                        pool.wait_ge(folded, b.t)
                    pool.tensor_copy(out, src).then_inc(summed_p, 1)
                else:
                    pool.tensor_tensor(out, out, src, ALU.add).then_inc(summed_p, 1)
            pool.wait_ge(summed_p, n_sums(t))
            pool.tensor_tensor(sum_p[:, :, 0, :], sum_p[:, :, 0, :], sum_p[:, :, 1, :], ALU.add
                               ).then_inc(folded_p, 1)

        def load(b):
            if b >= 2:
                pool.wait_ge(relu_added, b - 1)
            pool.dma_start(xe[b % 2].rearrange("p (t c) -> p t c", t=YT), x_v[b]).then_inc(xe_loaded[b % 2], 16)

        pool.wait_ge(z_added, NPAIR)
        load(0)
        load(1)
        for b in range(NY):
            pool.wait_ge(xe_loaded[b % 2], 16 * (b // 2 + 1))
            pool.wait_ge(e_ready, b + 1)
            g = acc[:, b * YT:(b + 1) * YT, :].rearrange(flat)
            pool.tensor_scalar(g, g, 0.0, None, ALU.max).then_inc(relu_made, 1)
            pool.wait_ge(relu_made, b + 1)
            pool.tensor_tensor(g, g, xe[b % 2], ALU.add).then_inc(relu_added, 1)
            if b + 2 < NY:
                load(b + 2)

    @block.scalar
    def _(act):
        def xt_high_part(b):
            act.wait_ge(xt_made, b + 1)
            if b >= 2:
                act.wait_ge(y_made, b - 1)
            act.activation(xtr[:, b % 2, :], ps_x[:, b % 2, :], ACT.Copy).then_inc(xt_high, 1)

        def y_high_part(b):
            act.wait_ge(y_made, b + 1)
            act.activation(zr[:, b * YT:(b + 1) * YT, :].rearrange(flat), ps_y[:, b % 2, :],
                           ACT.Copy).then_inc(y_high, 1)

        def a_high_part(b):
            act.wait_ge(raw_loaded[b.s], 16 * (b.n // RING + 1))
            if b.n_prod >= 2:
                act.wait_ge(block_done, b.n_prod - 1)
            act.activation(ar[:, b.n_prod % 2, :, :], raw[:, b.s, :, :], ACT.Copy).then_inc(a_high, 1)

        def degree_root(t):
            act.wait_ge(deg_inv, t + 1)
            act.activation(rs[:, 1, :], rs[:, 0, :], ACT.Sqrt).then_inc(deg_root, 1)

        def z_high_part(t):
            act.wait_ge(z_scaled, t + 1)
            act.activation(zr[:, t * PT:(t + 1) * PT, :], z[:, :, :], ACT.Copy).then_inc(z_high, 1)

        def exps(b):
            act.wait_ge(g_ready, b + 1)
            if b >= 2:
                act.wait_ge(x2_ready, b - 1)
            act.activation(ee[b % 2], acc[:, b * YT:(b + 1) * YT, :].rearrange(flat), ACT.Exp).then_inc(e_ready, 1)

        def row_root(pair):
            act.wait_ge(var2_inv, pair + 1)
            act.activation(rs[:, 1, :], rs[:, 0, :], ACT.Sqrt).then_inc(var2_root, 1)

        def turned_rows(pair):
            for q in range(BP):
                b = pair * BP + q
                act.wait_ge(xh_turned, b + 1)
                if pair:
                    act.wait_ge(logits_made, b - BP + 1)
                act.activation(xht[q], ps_x[:, q % 2, :], ACT.Copy).then_inc(xht_ready, 1)

        act.wait_ge(w_loaded, 16)
        act.activation(wr[:, :, :], w_raw[:, :, :], ACT.Copy).then_inc(w_high, 1)
        for b in range(NY + 2):
            if b < NY and b % BP == 0:
                act.wait_ge(var_inv, b // BP + 1)
                act.activation(rs[:, 1, :], rs[:, 0, :], ACT.Sqrt).then_inc(var_root, 1)
            if 1 <= b <= NY:
                xt_high_part(b - 1)
            if b >= 2:
                y_high_part(b - 2)
        for t, (before, after) in enumerate(steps):
            products = [b for b in before if b.multiplies]
            for b in products[:-2]:
                a_high_part(b)
            degree_root(t)
            for b in products[-2:-1]:
                a_high_part(b)
            z_high_part(t)
            for b in products[-1:]:
                a_high_part(b)
            for b in after:
                pair = b.ip - 1
                if t == last_t and b.ip:
                    if b.s == 0:
                        exps(pair * BP)
                        exps(pair * BP + 1)
                    if b.s == 2:
                        exps(pair * BP + 2)
                        exps(pair * BP + 3)
                    if b.s == 3:
                        a_high_part(b)
                        row_root(pair)
                        continue
                if t == last_t and b.ip >= 2 and b.s == 2:
                    turned_rows(b.ip - 2)
                a_high_part(b)
        turned_rows(NPAIR - 2)
        for q in range(BP):
            exps((NPAIR - 1) * BP + q)
        row_root(NPAIR - 1)
        turned_rows(NPAIR - 1)

    @block.vector
    def _(dve):
        chain = Chain(dve, v_step)
        step = chain.step

        def newton(out, a, r, tmp):
            step(dve.tensor_tensor(tmp, r, r, ALU.mult))
            step(dve.tensor_tensor(tmp, tmp, a, ALU.mult))
            step(dve.tensor_scalar(tmp, tmp, -0.5, 1.5, ALU.mult, ALU.add))
            step(dve.tensor_tensor(out, r, tmp, ALU.mult))

        def deviations(t, inv, root):
            for i in range(PT):
                last = dve.bn_stats(stats[:, i, :], acc[:, t * PT + i, :])
            step(last)
            for i in range(PT):
                last = dve.bn_aggr(mv[:, t * PT + i, :], stats[:, i, :])
            step(last)
            step(dve.tensor_scalar(rs[:, 2, :], mv[:, t * PT:(t + 1) * PT, 1], EPS, None, ALU.add))
            dve.reciprocal(rs[:, 0, :], rs[:, 2, :]).then_inc(inv, 1)
            dve.wait_ge(root, t + 1)
            newton(rs[:, 3, :], rs[:, 2, :], rs[:, 1, :], rs[:, 0, :])

        def normalise(b):
            for i in range(b * YT, (b + 1) * YT):
                last = dve.tensor_scalar(acc[:, i, :], acc[:, i, :], mv[:, i, 0:1], rs[:, 3, i % PT:i % PT + 1],
                                         ALU.subtract, ALU.mult)
            last.then_inc(xn_ready, 1)

        def xt_low_part(b):
            dve.wait_ge(xt_high, b + 1)
            dve.tensor_tensor(xtl[:, b % 2, :], ps_x[:, b % 2, :], xtr[:, b % 2, :].bitcast(F32),
                              ALU.subtract).then_inc(xt_low, 1)

        def y_low_part(b):
            dve.wait_ge(y_high, b + 1)
            rows_ = slice(b * YT, (b + 1) * YT)
            dve.tensor_tensor(zl[:, rows_, :].rearrange(flat), ps_y[:, b % 2, :],
                              zr[:, rows_, :].rearrange(flat).bitcast(F32), ALU.subtract).then_inc(y_low, 1)

        def sum_block(b):
            dve.wait_ge(raw_loaded[b.s], 16 * (b.n // RING + 1))
            out = sum_v[:, b.strip, :, :]
            src = raw[:, b.s, 0:2, :]
            if b.n_deg:
                dve.wait_ge(summed_v, b.n_deg)
            if b.jp == b.t and b.s % 2 == 0:
                if b.t:
                    dve.wait_ge(deg_made, b.t)
                dve.tensor_copy(out, src).then_inc(summed_v, 1)
            else:
                dve.tensor_tensor(out, out, src, ALU.add).then_inc(summed_v, 1)

        def fold(t):
            dve.wait_ge(summed_v, n_sums(t))
            step(dve.tensor_tensor(sum_v[:, :, 0, :], sum_v[:, :, 0, :], sum_v[:, :, 1, :], ALU.add))
            dve.wait_ge(folded_p, t + 1)
            dve.tensor_tensor(sum_v[:, :, 0, :], sum_v[:, :, 0, :], sum_p[:, :, 0, :], ALU.add).then_inc(folded, 1)

        pending = []
        strips = [0]

        def add_strip():
            b = pending.pop(0)
            dve.wait_ge(block_done, b.n_prod + 1)
            if strips[0]:
                dve.wait_ge(acc_added, strips[0])
            strips[0] += 1
            out = acc[:, b.i * SUB:(b.i + 1) * SUB, :]
            if b.kind == BOTH and b.jp == 0:
                dve.tensor_copy(out, ps_prod[:, b.strip, :, :]).then_inc(acc_added, 1)
            else:
                dve.tensor_tensor(out, ps_prod[:, b.strip, :, :], out, ALU.add).then_inc(acc_added, 1)

        def a_low_part(b):
            dve.wait_ge(a_high, b.n_prod + 1)
            k = b.n_prod % 2
            dve.tensor_tensor(al[:, k, :, :], raw[:, b.s, :, :], ar[:, k, :, :].bitcast(F32),
                              ALU.subtract).then_inc(a_low, 1)
            if pending and pending[0].n_prod + 2 <= b.n_prod:
                add_strip()
            if b.s % 2 == 1:
                pending.append(b)

        def z_whole(t):
            pair = slice(t * PT, (t + 1) * PT)
            if t:
                dve.wait_ge(z_added, t)
            step(dve.tensor_tensor(z[:, :, :], zr[:, pair, :].bitcast(F32), zl[:, pair, :].bitcast(F32), ALU.add))

        def degrees(t):
            dve.wait_ge(deg_made, t + 1)
            step(dve.tensor_scalar(rs[:, 2, :], ps_x[:, 0, 0:PT], 1.0, None, ALU.add))
            dve.reciprocal(rs[:, 0, :], rs[:, 2, :]).then_inc(deg_inv, 1)
            dve.wait_ge(deg_root, t + 1)
            newton(dinv[:, t * PT:(t + 1) * PT], rs[:, 2, :], rs[:, 1, :], rs[:, 0, :])
            for i in range(PT):
                last = dve.tensor_scalar(z[:, i, :], z[:, i, :], dinv[:, t * PT + i:t * PT + i + 1], None, ALU.mult)
            last.then_inc(z_scaled, 1)

        def z_low_part(t):
            dve.wait_ge(z_high, t + 1)
            pair = slice(t * PT, (t + 1) * PT)
            dve.tensor_tensor(zl[:, pair, :], z[:, :, :], zr[:, pair, :].bitcast(F32), ALU.subtract
                              ).then_inc(z_low, 1)

        def add_z(t):
            out = acc[:, t * PT:(t + 1) * PT, :]
            if strips[0]:
                dve.wait_ge(acc_added, strips[0])
            if t:
                dve.tensor_tensor(out, out, z[:, :, :], ALU.add).then_inc(z_added, 1)
            else:
                dve.tensor_copy(out, z[:, :, :]).then_inc(z_added, 1)
            dve.wait_ge(z_added, t + 1)

        def scale_rows(b):
            dve.wait_ge(acc_added, strips[0])
            for i in range(b * YT, (b + 1) * YT):
                last = dve.tensor_scalar(acc[:, i, :], acc[:, i, :], dinv[:, i:i + 1], None, ALU.mult)
            last.then_inc(g_ready, 1)

        def x2(b):
            dve.wait_ge(relu_added, b + 1)
            a = acc[:, b * YT:(b + 1) * YT, :].rearrange(flat)
            dve.scalar_tensor_tensor(a, ee[b % 2], 1.0, a, ALU.min, ALU.add).then_inc(x2_ready, 1)

        def normalise_rows(pair):
            for q in range(BP):
                b = pair * BP + q
                if pair:
                    dve.wait_ge(rows_stored[q], 16 * pair)
                    dve.wait_ge(xh_turned, b - BP + 1)
                for i in range(YT):
                    n = b * YT + i
                    last = dve.tensor_scalar(xh[q][:, i * C:(i + 1) * C], acc[:, n, :], mv[:, n, 0:1],
                                             rs[:, 3, n % PT:n % PT + 1], ALU.subtract, ALU.mult)
                last.then_inc(xh_ready, 1)

        def deviations2(pair):
            deviations(pair, var2_inv, var2_root)

        dve.wait_ge(w_high, 1)
        dve.tensor_tensor(wl[:, :, :], w_raw[:, :, :], wr[:, :, :].bitcast(F32), ALU.subtract).then_inc(w_low, 1)
        first = list(steps[0][0])
        for b in range(NY + 2):
            if b < NY and b % BP == 0:
                dve.wait_ge(x_loaded[b // BP], 16)
                deviations(b // BP, var_inv, var_root)
            if b < NY:
                normalise(b)
            if first:
                sum_block(first.pop(0))
            if 1 <= b <= NY:
                xt_low_part(b - 1)
            if b >= 2:
                y_low_part(b - 2)
        for t, (before, after) in enumerate(steps):
            if t:
                for b in before[:-4]:
                    sum_block(b)
                    if b.multiplies:
                        a_low_part(b)
                for b in before[-4:]:
                    sum_block(b)
            fold(t)
            tail = before[-4:] if t else [None] * 4
            for b in tail[:2]:
                if b:
                    a_low_part(b)
            z_whole(t)
            degrees(t)
            if t:
                a_low_part(tail[2])
            z_low_part(t)
            if t:
                a_low_part(tail[3])
            for b in after:
                pair = b.ip - 1
                if t == last_t and b.ip:
                    if b.s == 0:
                        scale_rows(pair * BP)
                        scale_rows(pair * BP + 1)
                    if b.s == 2:
                        scale_rows(pair * BP + 2)
                        scale_rows(pair * BP + 3)
                a_low_part(b)
                if b.ip == 0 and b.s == 1:
                    add_z(t)
                if t == last_t and b.ip:
                    if b.s == 0:
                        x2(pair * BP)
                    if b.s == 1:
                        x2(pair * BP + 1)
                    if b.s == 2:
                        x2(pair * BP + 2)
                        x2(pair * BP + 3)
                        dve.wait_ge(x2_ready, (pair + 1) * BP)
                    if b.s == 3:
                        deviations2(pair)
                        normalise_rows(pair)
        while pending:
            add_strip()
        for q in range(BP):
            scale_rows(last_t * BP + q)
        for q in range(BP):
            x2(last_t * BP + q)
        dve.wait_ge(x2_ready, NY)
        deviations2(last_t)
        normalise_rows(last_t)
        dve.wait_ge(logits_made, NY)
        dve.wait_ge(gate_loaded, 32)
        dve.tensor_tensor(lg[:, :, :], ps_gate, gb[:, :, :].broadcast_to([P, NT, E]), ALU.add).then_inc(lg_ready, 1)
        dve.wait_ge(lg_ready, 1)

    @block.tensor
    def _(pe):
        def transposes(b):
            pe.wait_ge(xn_ready, b + 1)
            if b >= 2:
                pe.wait_ge(xt_low, b - 1)
            for i in range(YT):
                for k in range(KC):
                    at_ = (i * KC + k) * P
                    last = pe.transpose(ps_x[:, b % 2, at_:at_ + P], acc[:, b * YT + i, k * P:(k + 1) * P], ident)
            last.then_inc(xt_made, 1)

        def y_tiles(b):
            pe.wait_ge(xt_low, b + 1)
            if b >= 2:
                pe.wait_ge(y_low, b - 1)
            for i in range(YT):
                for k in range(KC):
                    at_ = (i * KC + k) * P
                    hi, lo = (v[:, b % 2, at_:at_ + P] for v in (xtr, xtl))
                    for q, (lhs, rhs) in enumerate(((hi, wr), (hi, wl), (lo, wr))):
                        last = pe.matmul(ps_y[:, b % 2, i * C:(i + 1) * C], lhs, rhs[:, k, :],
                                         start=(i == 0 and k == 0 and q == 0), stop=(k == KC - 1 and q == 2),
                                         skip_group_check=True)
            last.then_inc(y_made, 1)

        def product_group(first, added, j_tile):
            for s in range(4):
                strip, half = s // 2, s % 2
                pe.wait_ge(a_low, first + (s + 1))
                if half == 0 and added is not None:
                    pe.wait_ge(acc_added, added + strip)
                for i in range(SUB):
                    for sub in range(SUB):
                        hi, lo = (v[:, s % 2, sub, i * P:(i + 1) * P] for v in (ar, al))
                        tile = j_tile + (half * SUB + sub)
                        mh, ml = (v[:, bass.ds(tile, 1), :].rearrange(flat) for v in (zr, zl))
                        for q, (lhs, rhs) in enumerate(((hi, mh), (hi, ml), (lo, mh))):
                            last = pe.matmul(ps_prod[:, strip, i, :], lhs, rhs,
                                             start=(half == 0 and i % 2 == 0 and sub == 0 and q == 0),
                                             stop=(half == 1 and sub == SUB - 1 and q == 2),
                                             skip_group_check=True)
                last.then_inc(block_done, 1)

        def degrees(t):
            pe.wait_ge(folded, t + 1)
            for i in range(PT):
                part = sum_v[:, i // SUB, 0, i % SUB * P:(i % SUB + 1) * P]
                last = pe.matmul(ps_x[:, 0, i:i + 1], part, ones[:, :], start=True, stop=True)
            last.then_inc(deg_made, 1)

        def row_logits(first):
            for q in range(BP + 1):
                if q < BP:
                    pe.wait_ge(xh_ready, first + (q + 1))
                    if q >= 2:
                        pe.wait_ge(xht_ready, first + (q - 1))
                    for m in range(YT * KC):
                        last = pe.transpose(ps_x[:, q % 2, m * P:(m + 1) * P], xh[q][:, m * P:(m + 1) * P], ident)
                    last.then_inc(xh_turned, 1)
                if q:
                    pe.wait_ge(xht_ready, first + q)
                    for i in range(YT):
                        out = ps_y[:, 0, bass.ds((first + (q - 1)) * (YT * E) + i * E, E)]
                        for k in range(KC):
                            m = i * KC + k
                            last = pe.matmul(out, xht[q - 1][:, m * P:(m + 1) * P], gw[:, k, :],
                                             start=(k == 0), stop=(k == KC - 1), skip_group_check=True)
                    last.then_inc(logits_made, 1)

        pe.wait_ge(w_low, 1)
        pe.wait_ge(ones_set, 1)
        pe.wait_ge(const_loaded, 16)
        for b in range(NY + 1):
            if b < NY:
                transposes(b)
            if b:
                y_tiles(b - 1)
        pe.wait_ge(y_low, NY)
        for t, (before, after) in enumerate(steps):
            lower = [b for b in before if b.multiplies]
            if t >= 2:
                base = lower[0].n_prod
                with pe.Fori(0, t - 1) as g:
                    product_group(g * 4 + base, g * 2 + (base // 2 - 1), g * PT)
            degrees(t)
            if t:
                base = lower[-4].n_prod
                product_group(base, base // 2 - 1, (t - 1) * PT)
            pe.wait_ge(z_low, t + 1)
            base = after[0].n_prod
            if t == 0:
                product_group(base, None, 0)
            elif t < last_t:
                with pe.Fori(0, t + 1) as g:
                    product_group(g * 4 + base, g * 2 + (base // 2 - 1), t * PT)
            else:
                pe.wait_ge(gate_loaded, 32)
                product_group(base, base // 2 - 1, t * PT)
                with pe.Fori(0, t) as g:
                    product_group(g * 4 + (base + 4), g * 2 + (base // 2 + 1), t * PT)
                    row_logits(g * BP)
                row_logits(last_t * BP)


def route(nc, ctx, w1, w2, consts, at, lg, wts, ids, dst, tile_expert, w1r, w1l, w2r, w2l):

    def sb(name, shape, dt=F32):
        return ctx.enter_context(nc.sbuf_tensor(name, shape, dt))

    def ps(name, shape):
        return ctx.enter_context(nc.psum_tensor(name, shape, F32))

    def sem(name):
        return ctx.enter_context(nc.semaphore(name))

    stage = sb("stage", [P, 2, KC * F])

    ps_cnt = ps("ps_cnt", [P, NT, E])
    ps_tot = ps("ps_tot", [P, NT, E])
    ps_ids = ps("ps_ids", [P, 2, SLOTS])

    v_chain = sem("v_chain2")
    stage_loaded = [sem(f"stage_loaded{i}") for i in range(2)]
    w_hi = sem("w_hi")
    w_lo = sem("w_lo")
    diff_ready = sem("diff_ready")
    exp_ready = sem("exp_ready")
    mask_ready = sem("mask_ready")
    counts_ready = sem("counts_ready")
    hot_ready = sem("hot_ready")
    hot_used = sem("hot_used")
    ids_made = sem("ids_made")

    l2 = sb("l2", [P, NT, E])
    cand = sb("cand", [P, NT, E])
    hot1 = sb("hot1", [P, NT, E])
    hot2 = sb("hot2", [P, NT, E])
    mask = sb("mask", [P, NT, E])
    col = sb("col", [P, 8, NT])
    tot = sb("tot", [P, E, NT])
    keep = sb("keep", [P, E, NT])
    incl = sb("incl", [P, E, NT])
    ex = sb("ex", [P, 6, E])
    ti = sb("ti", [P, SLOTS, E])
    tf = sb("tf", [P, SLOTS])
    pos = sb("pos", [P, CW])
    pos_i = sb("pos_i", [P, 2, CW], I32)
    pos_f = sb("pos_f", [P, 2, CW])
    hot_r = sb("hot_r", [P, 4, P], BF16)
    hot_q = sb("hot_q", [P, 4, 2, SLOTS], BF16)
    ones = sb("ones2", [P, P])
    lane_b = sb("lane_b", [P, P], BF16)
    tile_b = sb("tile_b", [P, SLOTS], BF16)
    v = sb("v", [P, SLOTS])
    pad = sb("pad", [P, SLOTS])
    ones2_set = sem("ones2_set")

    def K(name):
        return consts[:, at[name]]

    def chunks():
        for e in range(E):
            yield w1[e].rearrange("(k p) f -> p k f", p=P), w1r[:, e], w1l[:, e]
        for e in range(E):
            yield w2[e].rearrange("(k p) c -> p k c", p=P), w2r[:, e], w2l[:, e]

    block = ctx.enter_context(nc.Block())

    @block.gpsimd
    def _(pool):
        pool.memset(ones[:, :], 1.0).then_inc(ones2_set, 1)
        pool.memset(keep[:, :, :], 1.0).then_inc(ones2_set, 1)
        pool.wait_ge(ones2_set, 2)
        pool.memset(keep[:, :, 0:1], 0.0).then_inc(ones2_set, 1)
        for n, (src, hi, lo) in enumerate(chunks()):
            def load(m, s):
                pool.dma_start(stage[:, m % 2, :].rearrange("p (k f) -> p k f", k=s.shape[1]), s
                               ).then_inc(stage_loaded[m % 2], 16)
            if n == 0:
                todo = [c[0] for c in chunks()]
                load(0, todo[0])
                load(1, todo[1])
            pool.wait_ge(w_hi, n + 1)
            pool.tensor_tensor(lo.rearrange("p k f -> p (k f)"), stage[:, n % 2, :],
                               hi.rearrange("p k f -> p (k f)").bitcast(F32), ALU.subtract).then_inc(w_lo, 1)
            if n + 2 < 2 * E:
                pool.wait_ge(w_lo, n + 1)
                load(n + 2, todo[n + 2])

    @block.scalar
    def _(act):
        def weights(n):
            hi = list(chunks())[n][1]
            act.wait_ge(stage_loaded[n % 2], 16 * (n // 2 + 1))
            act.activation(hi.rearrange("p k f -> p (k f)"), stage[:, n % 2, :], ACT.Copy).then_inc(w_hi, 1)

        for n in range(2 * E):
            weights(n)
            if n == 0:
                act.wait_ge(diff_ready, 1)
                act.activation(col[:, 3, :], col[:, 2, :], ACT.Exp).then_inc(exp_ready, 1)

    @block.vector
    def _(dve):
        ch = Chain(dve, v_chain)
        step = ch.step

        def over_e(ap):
            return ap.unsqueeze(2).broadcast_to([P, NT, E])

        def over_t(ap):
            return ap.unsqueeze(1).broadcast_to([P, NT, E])

        dve.tensor_copy(lane_b[:, :], K("lane"))
        step(dve.tensor_copy(tile_b[:, :], K("tile")))
        idx = over_t(K("expert"))

        def pick(src, top, hot):
            step(dve.tensor_reduce(top, src, AX.X, ALU.max))
            step(dve.tensor_tensor(cand[:, :, :], src, over_e(top), ALU.is_equal))
            step(dve.scalar_tensor_tensor(cand[:, :, :], cand[:, :, :], -float(E), idx, ALU.mult, ALU.add))
            step(dve.tensor_reduce(col[:, 7, :], cand[:, :, :], AX.X, ALU.min))
            step(dve.tensor_tensor(hot, cand[:, :, :], over_e(col[:, 7, :]), ALU.is_equal))

        pick(lg[:, :, :], col[:, 0, :], hot1[:, :, :])
        step(dve.scalar_tensor_tensor(l2[:, :, :], hot1[:, :, :], -FAR, lg[:, :, :], ALU.mult, ALU.add))
        pick(l2[:, :, :], col[:, 1, :], hot2[:, :, :])
        dve.tensor_tensor(col[:, 2, :], col[:, 1, :], col[:, 0, :], ALU.subtract).then_inc(diff_ready, 1)
        dve.tensor_tensor(mask[:, :, :], hot1[:, :, :], hot2[:, :, :], ALU.add).then_inc(mask_ready, 1)
        dve.wait_ge(exp_ready, 1)
        step(dve.tensor_scalar(col[:, 4, :], col[:, 3, :], 1.0, None, ALU.add))
        step(dve.reciprocal(wts[:, 0, :], col[:, 4, :]))
        step(dve.tensor_tensor(wts[:, 1, :], wts[:, 0, :], col[:, 3, :], ALU.mult))
        dve.wait_ge(counts_ready, 1)
        dve.wait_ge(ones2_set, 3)
        step(dve.tensor_copy(tot[:, :, :], ps_tot[:, :, :].rearrange("p t e -> p e t")))
        step(dve.tensor_tensor_scan(incl[:, :, :].rearrange("p e t -> p (e t)"),
                                    keep[:, :, :].rearrange("p e t -> p (e t)"),
                                    tot[:, :, :].rearrange("p e t -> p (e t)"), 0.0, ALU.mult, ALU.add))
        rows_e = incl[:, :, NT - 1:NT].broadcast_to([P, E, NT])
        full = cand[:, :, :].rearrange("p t e -> p (t e)").rearrange("p (e t) -> p e t", e=E)
        step(dve.tensor_tensor(full, rows_e, K("step").unsqueeze(1).broadcast_to([P, E, NT]), ALU.is_gt))
        step(dve.tensor_reduce(ex[:, 0, :], full, AX.X, ALU.add))
        step(dve.tensor_tensor_scan(ex[:, 1, :], ones[:, 0:E], ex[:, 0, :], 0.0, ALU.mult, ALU.add))
        step(dve.tensor_tensor(ex[:, 2, :], ex[:, 1, :], ex[:, 0, :], ALU.subtract))
        step(dve.tensor_scalar(ex[:, 3, :], ex[:, 2, :], float(P), None, ALU.mult))
        step(dve.tensor_tensor(incl[:, :, :], incl[:, :, :], tot[:, :, :], ALU.subtract))
        step(dve.tensor_tensor(incl[:, :, :], incl[:, :, :], ex[:, 3, :].unsqueeze(2).broadcast_to([P, E, NT]),
                               ALU.add))
        step(dve.tensor_tensor(l2[:, :, :], ps_cnt[:, :, :], incl[:, :, :].rearrange("p e t -> p t e"), ALU.add))
        for k, hot in enumerate((hot1, hot2)):
            step(dve.tensor_tensor(cand[:, :, :], hot[:, :, :], l2[:, :, :], ALU.mult))
            step(dve.tensor_reduce(pos[:, k * NT:(k + 1) * NT], cand[:, :, :], AX.X, ALU.add))
        step(dve.tensor_copy(pos_i[:, 0, :], pos[:, :]))
        step(dve.tensor_scalar(pos_i[:, 1, :], pos_i[:, 0, :], P - 1, None, ALU.bitwise_and))
        step(dve.tensor_copy(pos_f[:, 1, :], pos_i[:, 1, :]))
        step(dve.tensor_tensor(pos_f[:, 0, :], pos[:, :], pos_f[:, 1, :], ALU.subtract))
        step(dve.tensor_scalar(pos_f[:, 0, :], pos_f[:, 0, :], 1.0 / P, None, ALU.mult))

        def hots(c, k):
            if not isinstance(c, int) or c >= 4:
                dve.wait_ge(hot_used, c - 3)
            q, r = pos_f[:, 0, bass.ds(c, 1)], pos_f[:, 1, bass.ds(c, 1)]
            dve.tensor_scalar(hot_r[:, k, :], lane_b[:, :], r, None, ALU.is_equal)
            dve.tensor_scalar(hot_q[:, k, 0, :], tile_b[:, :], q, consts[:, bass.ds(c + at["column"].start, 1)],
                              ALU.is_equal, ALU.mult)
            dve.tensor_scalar(hot_q[:, k, 1, :], tile_b[:, :], q, K("row"),
                              ALU.is_equal, ALU.mult).then_inc(hot_ready, 1)

        for c in range(4):
            hots(c, c)
        with dve.Fori(1, CW // 4) as i:
            for c in range(4):
                hots(i * 4 + c, c)
        step(dve.tensor_tensor(ti[:, :, :], ex[:, 1:2, :].broadcast_to([P, SLOTS, E]),
                               K("tile").unsqueeze(2).broadcast_to([P, SLOTS, E]), ALU.is_le))
        step(dve.tensor_reduce(tf[:, :], ti[:, :, :], AX.X, ALU.add))
        step(dve.tensor_scalar(tile_expert[:, :], tf[:, :], float(E - 1), None, ALU.min))
        dve.wait_ge(ids_made, 1)
        step(dve.tensor_scalar(v[:, :], ps_ids[:, 0, :], float(P), -float(P), ALU.mult, ALU.add))
        step(dve.tensor_tensor(v[:, :], v[:, :], ps_ids[:, 1, :], ALU.add))
        step(dve.tensor_scalar(pad[:, :], v[:, :], 0.0, None, ALU.is_lt))
        step(dve.tensor_scalar(tf[:, :], K("row").broadcast_to([P, SLOTS]), float(PAD_ROW + P), None, ALU.add))
        step(dve.tensor_tensor(tf[:, :], tf[:, :], pad[:, :], ALU.mult))
        step(dve.tensor_tensor(dst[:, :], tf[:, :], v[:, :], ALU.add))
        step(dve.tensor_scalar(tf[:, :], v[:, :], float(N), -float(N), ALU.is_ge, ALU.mult))
        step(dve.tensor_scalar(v[:, :], v[:, :], 0.0, None, ALU.max))
        step(dve.tensor_tensor(ids[:, :], tf[:, :], v[:, :], ALU.add))

    @block.tensor
    def _(pe):
        pe.wait_ge(mask_ready, 1)
        pe.wait_ge(ones2_set, 1)
        flat = mask[:, :, :].rearrange("p t e -> p (t e)")
        pe.matmul(ps_cnt[:, :, :].rearrange("p t e -> p (t e)"), K("before"), flat, start=True, stop=True)
        pe.matmul(ps_tot[:, :, :].rearrange("p t e -> p (t e)"), ones[:, :], flat, start=True,
                  stop=True).then_inc(counts_ready, 1)

        def place(c, k):
            pe.wait_ge(hot_ready, c + 1)
            return pe.matmul(ps_ids[:, :, :].rearrange("p h q -> p (h q)"), hot_r[:, k, :],
                             hot_q[:, k, :, :].rearrange("p h q -> p (h q)"),
                             start=(isinstance(c, int) and c == 0), stop=False, skip_group_check=True
                             ).then_inc(hot_used, 1)

        for c in range(4):
            place(c, c)
        with pe.Fori(1, CW // 4) as i:
            for c in range(4):
                place(i * 4 + c, c)
        pe.wait_ge(hot_used, CW)
        pe.nop().then_inc(ids_made, 1)


def experts(nc, ctx, b1, b2, rows, parts, consts, at, ids, dst, tile_expert, w1r, w1l, w2r, w2l):

    def sb(name, shape, dt=F32):
        return ctx.enter_context(nc.sbuf_tensor(name, shape, dt))

    def ps(name, shape):
        return ctx.enter_context(nc.psum_tensor(name, shape, F32))

    def sem(name):
        return ctx.enter_context(nc.semaphore(name))

    RG = 4
    b1a = sb("b1a", [P, E, F])
    b2a = sb("b2a", [P, E, C])
    xg = sb("xg", [P, RG, C])
    xgr = sb("xgr", [P, C], F32R)
    xgl = sb("xgl", [P, C], F32R)
    h = sb("h", [P, F])
    hr = sb("hr", [P, 2, F], F32R)
    hl = sb("hl", [P, 2, F], F32R)
    yo = sb("yo", [P, 2, C])

    ps_h = ps("ps_h", [P, 2, F])
    ps_xt = ps("ps_xt", [P, 1, BW])
    ps_ht = ps("ps_ht", [P, 2, F])
    ps_o = ps("ps_o", [P, 2, BW])

    b_loaded = sem("b_loaded")
    xg_loaded = [sem(f"xg_loaded{i}") for i in range(RG)]
    yo_stored = [sem(f"yo_stored{i}") for i in range(2)]
    xg_turned = sem("xg_turned")
    xg_high = sem("xg_high")
    xg_low = sem("xg_low")
    h_made = sem("h_made")
    h_ready = sem("h_ready")
    h_turned = sem("h_turned")
    h_high = sem("h_high")
    h_low = sem("h_low")
    o_made = sem("o_made")
    o_ready = sem("o_ready")

    block = ctx.enter_context(nc.Block())

    def is_int(q):
        return isinstance(q, int)

    def stages(eng, stage):
        bodies = (SLOTS - 4) // 4
        for q in range(-1, 3):
            stage(q, q % 4)
        with eng.Fori(0, bodies) as i:
            for n in range(3, 7):
                stage(i * 4 + n, n % 4)
        for q in range(3 + 4 * bodies, SLOTS + 1):
            stage(q, q % 4)

    @block.sync
    def _(sp):
        sp.dma_start(b1a[:, :, :], b1.rearrange("e f -> (e f)").partition_broadcast(P)).then_inc(b_loaded, 16)
        sp.dma_start(b2a[:, :, :], b2.rearrange("e f -> (e f)").partition_broadcast(P)).then_inc(b_loaded, 16)

    @block.gpsimd
    def _(pool):
        def gather(q):
            if q >= RG:
                pool.wait_ge(xg_turned, q - RG + 1)
            pool.indirect_dma_start(xg[:, q % RG, :], None, rows,
                                    bass.IndirectOffsetOnAxis(ap=ids[:, q:q + 1].bitcast(U32), axis=0)
                                    ).then_inc(xg_loaded[q % RG], 16)

        def scatter(q):
            pool.wait_ge(o_ready, q + 1)
            if q >= 1:
                pool.wait_ge(yo_stored[1 - q % 2], 16 * ((q + 1) // 2))
            pool.indirect_dma_start(parts,
                                    bass.IndirectOffsetOnAxis(ap=dst[:, q:q + 1].bitcast(U32), axis=0),
                                    yo[:, q % 2, :], None).then_inc(yo_stored[q % 2], 16)

        for q in range(RG):
            gather(q)
        for q in range(SLOTS):
            scatter(q)
            if q + RG < SLOTS:
                gather(q + RG)
        pool.wait_ge(yo_stored[0], 16 * ((SLOTS + 1) // 2))
        pool.wait_ge(yo_stored[1], 16 * (SLOTS // 2))

    @block.scalar
    def _(act):
        def stage(q, k4):
            k = k4 % 2
            if not is_int(q) or q + 1 < SLOTS:
                act.wait_ge(xg_turned, q + 2)
                if not is_int(q) or q >= 0:
                    act.wait_ge(h_made, q + 1)
                act.activation(xgr[:, :], ps_xt[:, 0, 0:C], ACT.Copy).then_inc(xg_high, 1)
            if not is_int(q) or 0 <= q < SLOTS:
                act.wait_ge(h_turned, q + 1)
                if not is_int(q) or q >= 2:
                    act.wait_ge(o_made, q - 1)
                act.activation(hr[:, k, :], ps_ht[:, k, :], ACT.Relu).then_inc(h_high, 1)

        stages(act, stage)

    @block.vector
    def _(dve):
        dve.wait_ge(b_loaded, 32)

        def stage(q, k4):
            k = k4 % 2
            if not is_int(q) or 0 <= q < SLOTS:
                e = dve.value_load(tile_expert[0:1, bass.ds(q, 1)], min_val=0, max_val=E - 1)
                dve.wait_ge(h_made, q + 1)
                if not is_int(q) or q >= 1:
                    dve.wait_ge(h_turned, q)
                dve.tensor_tensor(h[:, :], ps_h[:, k, :], b1a[:, bass.ds(e, 1), :].rearrange("p e f -> p (e f)"),
                                  ALU.add).then_inc(h_ready, 1)
            if not is_int(q) or q + 1 < SLOTS:
                dve.wait_ge(xg_high, q + 2)
                dve.tensor_tensor(xgl[:, :], ps_xt[:, 0, 0:C], xgr[:, :].bitcast(F32),
                                  ALU.subtract).then_inc(xg_low, 1)
            if not is_int(q) or 0 <= q < SLOTS:
                dve.wait_ge(h_high, q + 1)
                dve.scalar_tensor_tensor(hl[:, k, :], ps_ht[:, k, :], 0.0, hr[:, k, :].bitcast(F32),
                                         ALU.max, ALU.subtract).then_inc(h_low, 1)
            if not is_int(q) or q >= 1:
                e = dve.value_load(tile_expert[0:1, bass.ds(q - 1, 1)], min_val=0, max_val=E - 1)
                dve.wait_ge(o_made, q)
                if not is_int(q) or q >= 3:
                    dve.wait_ge(yo_stored[1 - k], q * 8 - (8 if k else 16))
                dve.tensor_tensor(yo[:, 1 - k, :], ps_o[:, 1 - k, 0:C],
                                  b2a[:, bass.ds(e, 1), :].rearrange("p e f -> p (e f)"),
                                  ALU.add).then_inc(o_ready, 1)

        stages(dve, stage)

    @block.tensor
    def _(pe):
        ident = consts[:, at["ident"]]

        def stage(q, k4):
            k = k4 % 2
            if not is_int(q) or 0 <= q < SLOTS:
                e = pe.value_load(tile_expert[0:1, bass.ds(q, 1)], min_val=0, max_val=E - 1)
                pe.wait_ge(xg_low, q + 1)
                if not is_int(q) or q >= 2:
                    pe.wait_ge(h_ready, q - 1)
                for c in range(KC):
                    hi, lo = xgr[:, c * P:(c + 1) * P], xgl[:, c * P:(c + 1) * P]
                    mh, ml = (v[:, bass.ds(e, 1), c, :].rearrange("p e f -> p (e f)") for v in (w1r, w1l))
                    for n, (lhs, rhs) in enumerate(((hi, mh), (hi, ml), (lo, mh))):
                        last = pe.matmul(ps_h[:, k, :], lhs, rhs, start=(c == 0 and n == 0),
                                         stop=(c == KC - 1 and n == 2))
                last.then_inc(h_made, 1)
            if not is_int(q) or q + 1 < SLOTS:
                n = q + 1
                g = (k4 + 1) % RG
                pe.wait_ge(xg_loaded[g], n * 4 + (16 - 4 * g))
                if not is_int(q) or q >= 0:
                    pe.wait_ge(xg_low, n)
                for c in range(KC):
                    last = pe.transpose(ps_xt[:, 0, c * P:(c + 1) * P], xg[:, g, c * P:(c + 1) * P], ident)
                last.then_inc(xg_turned, 1)
            if not is_int(q) or q >= 1:
                e = pe.value_load(tile_expert[0:1, bass.ds(q - 1, 1)], min_val=0, max_val=E - 1)
                pe.wait_ge(h_low, q)
                if not is_int(q) or q >= 3:
                    pe.wait_ge(o_ready, q - 2)
                for c in range(KF):
                    hi, lo = hr[:, 1 - k, c * P:(c + 1) * P], hl[:, 1 - k, c * P:(c + 1) * P]
                    mh, ml = (v[:, bass.ds(e, 1), c, :].rearrange("p e f -> p (e f)") for v in (w2r, w2l))
                    for n, (lhs, rhs) in enumerate(((hi, mh), (hi, ml), (lo, mh))):
                        last = pe.matmul(ps_o[:, 1 - k, 0:C], lhs, rhs, start=(c == 0 and n == 0),
                                         stop=(c == KF - 1 and n == 2))
                last.then_inc(o_made, 1)
            if not is_int(q) or 0 <= q < SLOTS:
                pe.wait_ge(h_ready, q + 1)
                if not is_int(q) or q >= 2:
                    pe.wait_ge(h_low, q - 1)
                for c in range(KF):
                    last = pe.transpose(ps_ht[:, k, c * P:(c + 1) * P], h[:, c * P:(c + 1) * P], ident)
                last.then_inc(h_turned, 1)

        stages(pe, stage)


def combine(nc, ctx, parts, out, acc, wts):

    def sem(name):
        return ctx.enter_context(nc.semaphore(name))

    CT = 4
    y = ctx.enter_context(nc.sbuf_tensor("y", [P, 2, 2, CT, C], F32))
    o = ctx.enter_context(nc.sbuf_tensor("o", [P, 2, CT, C], F32))
    y_loaded = [sem(f"y_loaded{i}") for i in range(2)]
    o_stored = [sem(f"o_stored{i}") for i in range(2)]
    second = sem("second")
    first_added = sem("first_added")
    out_ready = sem("out_ready")
    parts_v = parts[0:2 * N, :].rearrange("(k b t p) c -> k b p t c", k=2, t=CT, p=P)
    out_v = out.rearrange("(b t p) c -> b p t c", t=CT, p=P)
    NBATCH = NT // CT

    def store(act, b):
        act.wait_ge(out_ready, b + 1)
        act.dma_start(out_v[b], o[:, b % 2, :, :]).then_inc(o_stored[b % 2], 16)

    block = ctx.enter_context(nc.Block())

    @block.sync
    def _(sp):
        for b in range(NBATCH):
            if b >= 2:
                sp.wait_ge(out_ready, b - 1)
            for k in range(2):
                sp.dma_start(y[:, b % 2, k, :, :], parts_v[k, b]).then_inc(y_loaded[b % 2], 16)

    @block.scalar
    def _(act):
        for b in range(NBATCH):
            act.wait_ge(y_loaded[b % 2], 32 * (b // 2 + 1))
            if b >= 2:
                act.wait_ge(o_stored[b % 2], 16 * (b // 2))
            for i in range(CT):
                last = act.activation(o[:, b % 2, i, :], y[:, b % 2, 1, i, :], ACT.Copy, bias=-1.0,
                                      scale=wts[:, 1, b * CT + i:b * CT + i + 1])
            last.then_inc(second, 1)
            if b:
                store(act, b - 1)
        store(act, NBATCH - 1)
        for k in range(2):
            act.wait_ge(o_stored[k], 16 * (NBATCH // 2))

    @block.vector
    def _(dve):
        for b in range(NBATCH):
            dve.wait_ge(y_loaded[b % 2], 32 * (b // 2 + 1))
            for i in range(CT):
                t = b * CT + i
                last = dve.scalar_tensor_tensor(acc[:, t, :], y[:, b % 2, 0, i, :], wts[:, 0, t:t + 1],
                                                acc[:, t, :], ALU.mult, ALU.add)
            last.then_inc(first_added, 1)
            dve.wait_ge(first_added, b + 1)
            dve.wait_ge(second, b + 1)
            ov = o[:, b % 2, :, :]
            dve.tensor_tensor(ov, ov, acc[:, b * CT:(b + 1) * CT, :], ALU.add).then_inc(out_ready, 1)


def graph_then_experts(nc, x, adj, w, gate_w, gate_b, w1, b1, w2, b2, const, out):
    at, width = const_slices()
    rows = nc.dram_tensor("rows", [N, C], F32, kind="Internal").ap()
    parts = nc.dram_tensor("parts", [2 * N + P, C], F32, kind="Internal").ap()
    with ExitStack() as whole:
        def sb(ctx, name, shape, dt=F32):
            return ctx.enter_context(nc.sbuf_tensor(name, shape, dt))

        consts = sb(whole, "consts", [P, width])
        lg = sb(whole, "lg", [P, NT, E])
        wts = sb(whole, "wts", [P, 2, NT])
        ids = sb(whole, "ids", [P, SLOTS], I32)
        dst = sb(whole, "dst", [P, SLOTS], I32)
        tile_expert = sb(whole, "tile_expert", [P, SLOTS], I32)
        acc = sb(whole, "acc", [P, NT, C])
        with ExitStack() as ctx:
            graph_layer(nc, ctx, x, adj, w, gate_w, gate_b, const, rows, consts, at, acc, lg)
        with ExitStack() as weights:
            w1r, w1l = (sb(weights, n, [P, E, KC, F], F32R) for n in ("w1r", "w1l"))
            w2r, w2l = (sb(weights, n, [P, E, KF, C], F32R) for n in ("w2r", "w2l"))
            with ExitStack() as ctx:
                route(nc, ctx, w1, w2, consts, at, lg, wts, ids, dst, tile_expert, w1r, w1l, w2r, w2l)
            with ExitStack() as ctx:
                experts(nc, ctx, b1, b2, rows, parts, consts, at, ids, dst, tile_expert, w1r, w1l, w2r, w2l)
        with ExitStack() as ctx:
            combine(nc, ctx, parts, out, acc, wts)


def constants():
    import numpy as np
    lane = np.arange(P)
    table = dict(ident=np.eye(P), before=lane[:, None] < lane[None, :], lane=lane, tile=np.arange(SLOTS),
                 expert=np.arange(E), step=P * np.arange(NT), column=1 + np.arange(CW), row=lane[:, None])
    parts = [np.broadcast_to(table[name], (P, width)) for name, width in WIDTHS.items()]
    return np.ascontiguousarray(np.concatenate(parts, 1).astype(np.float32))


def kernel(**inputs):
    import numpy as np
    import concourse.bacc as bacc
    from concourse.bass_utils import run_bass_kernel_spmd as run

    nc = bacc.Bacc("TRN2", target_bir_lowering=False, num_devices=1)
    a = {name: np.ascontiguousarray(v) for name, v in inputs.items()}
    blocks = a["adj"].T.reshape(NB, SUB, P, NB, BW).transpose(0, 3, 2, 1, 4)
    arrays = {
        "x_in": a["x"], "adj_in": np.ascontiguousarray(blocks), "w_in": a["L0_gnn_w"],
        "gate_w_in": a["L0_ffn_gate_w"], "gate_b_in": a["L0_ffn_gate_b"], "w1_in": a["L0_ffn_w1"],
        "b1_in": a["L0_ffn_b1"], "w2_in": a["L0_ffn_w2"], "b2_in": a["L0_ffn_b2"], "const_in": constants(),
    }
    args = [nc.dram_tensor(name, v.shape, mybir.dt.from_np(v.dtype), kind="ExternalInput").ap()
            for name, v in arrays.items()]
    args.append(nc.dram_tensor("out_0", (N, C), F32, kind="ExternalOutput").ap())
    graph_then_experts(nc, *args)
    r = run(nc, [arrays], core_ids=[0])
    return r.results[0]["out_0"]
```

```python
from contextlib import ExitStack

import concourse.bass as bass
from concourse import mybir

F32 = mybir.dt.float32
F32R = mybir.dt.float32r
BF16 = mybir.dt.bfloat16
I32 = mybir.dt.int32
U32 = mybir.dt.uint32
ALU = mybir.AluOpType
ACT = mybir.ActivationFunctionType
AX = mybir.AxisListType

P = 128
N = 4096
C = 256
KC = C // P
NT = N // P
BW = 512
SUB = BW // P
NB = N // BW
NPAIR = NB // 2
PT = 2 * SUB
RING = 4
EARLY = 6
SUM_LAG = 3
YT = 2
NY = NT // YT
EPS = 1e-5
E = 8
F = 512
KF = F // P
SLOTS = 2 * NT + E - 1
PAD_ROW = 2 * N
FAR = 3.0e38
CW = 2 * NT

WIDTHS = dict(ident=P, before=P, lane=P, tile=SLOTS, expert=E, step=NT, column=CW, row=1)

DEG, BOTH, PROD = "deg", "both", "prod"


def plan():
    deg = [[(DEG, jp, t, s) for jp in range(t, NPAIR) for s in range(4)] for t in range(NPAIR)] + [[]]
    steps = []
    left = deg[0]
    for t in range(NPAIR):
        both = [(BOTH, jp, t, s) for jp in range(t) for s in range(4)]
        if t < 2:
            before = spread(both, left[:4]) + left[4:] if t else left
        else:
            before = spread(both[:-4], left) + both[-4:]
        ahead = deg[t + 1]
        now = (4, len(ahead) // 2, len(ahead), 0)[t]
        after = spread([(PROD, t, ip, s) for ip in range(t + 1) for s in range(4)], ahead[:now])
        left = ahead[now:]
        steps.append((before, after))
    return steps


def spread(pieces, others):
    out, k = [], 0
    for n, piece in enumerate(pieces):
        out.append(piece)
        while k < len(others) and (k + 1) * len(pieces) <= (n + 1) * len(others):
            out.append(others[k])
            k += 1
    return out


def const_slices():
    at, out = 0, {}
    for name, width in WIDTHS.items():
        out[name] = slice(at, at + width)
        at += width
    return out, at


class Chain:

    def __init__(self, eng, sem):
        self.eng, self.sem, self.n = eng, sem, 0

    def step(self, ins):
        self.n += 1
        ins.then_inc(self.sem, 1)
        self.eng.wait_ge(self.sem, self.n)


class Block:

    def __init__(self, n, kind, t, jp, ip, s, n_deg, n_both, n_prod):
        self.n, self.kind, self.t, self.jp, self.ip, self.s = n, kind, t, jp, ip, s
        self.j, self.strip, self.i = 2 * jp + s % 2, s // 2, 2 * ip + s // 2
        self.slot, self.load = n % RING, n // RING + 1
        self.multiplies = kind != DEG
        self.n_deg, self.n_both, self.n_prod = n_deg, n_both, n_prod
        self.halved = kind == DEG and ip == 0 and (jp, s) != (NPAIR - 1, 3)


def blocks_of(steps):
    out, n, n_deg, n_both, n_prod = [], 0, 0, 0, 0
    for t, parts in enumerate(steps):
        both = []
        for part in parts:
            row = []
            for kind, jp, ip, s in part:
                row.append(Block(n, kind, t, jp, ip, s, n_deg, n_both, n_prod))
                n += 1
                n_deg += kind == DEG
                n_both += kind == BOTH
                n_prod += kind != DEG
            both.append(row)
        out.append(both)
    return out


def graph_layer(nc, ctx, x, adj, adj_rows, w, gate_w, gate_b, const, rows, consts, at_const, acc, lg,
                weights):
    steps = blocks_of(plan())
    every = [b for step in steps for part in step for b in part]
    at = {b.n: b for b in every}
    last_t = NPAIR - 1

    def sb(name, shape, dt=F32):
        return ctx.enter_context(nc.sbuf_tensor(name, shape, dt))

    def ps(name, shape):
        return ctx.enter_context(nc.psum_tensor(name, shape, F32))

    def sem(name):
        return ctx.enter_context(nc.semaphore(name))

    w1r, w1l, w2l = weights.w1r, weights.w1l, weights.w2l
    zr = w1r.rearrange("p e k f -> p (e k f)").rearrange("p (t c) -> p t c", c=C)
    zl = w1l.rearrange("p e k f -> p (e k f)").rearrange("p (t c) -> p t c", c=C)
    z = sb("z", [P, PT, C])
    raw = sb("raw", [P, RING, SUB, BW])
    parts_a = w2l.rearrange("p e k c -> p (e k c)").rearrange("p (h n a i) -> p h n a i", h=2, n=2, a=SUB)
    ar, al = parts_a[:, 0], parts_a[:, 1]
    sum_a = sb("sum_a", [P, NT, NPAIR])
    sum_v = sb("sum_v", [P, 2, 2, BW])
    sum_p = sb("sum_p", [P, 2, 2, BW])
    w_raw = sb("w_raw", [P, KC, C])
    wr = sb("wr", [P, KC, C], F32R)
    wl = sb("wl", [P, KC, C], F32R)
    xtr = sb("xtr", [P, 2, YT * C], F32R)
    xtl = sb("xtl", [P, 2, YT * C], F32R)
    ones = sb("ones", [P, 1])
    stats = sb("stats", [P, PT, 6])
    mv = sb("mv", [P, NT, 2])
    rs = sb("rs", [P, 3, PT])
    rstd = sb("rstd", [P, NT])
    dinv = sb("dinv", [P, NT])
    gw = sb("gw", [P, KC, E])
    gb = sb("gb", [P, 1, E])
    flat = "p t c -> p (t c)"
    xe = [z[:, YT * k:YT * (k + 1), :].rearrange(flat) for k in range(2)]
    ee = [z[:, YT * (k + 2):YT * (k + 3), :].rearrange(flat) for k in range(2)]
    ee_end = ee + xe
    tail_slot = every[-4].slot
    x_end = raw[:, tail_slot, :, :]
    early = [raw[:, (tail_slot + 1 + n // 2) % RING, 2 * (n % 2):2 * (n % 2) + 2, :].rearrange("p a i -> p (a i)")
             for n in range(EARLY)]
    xh = [sum_v[:, k // 2, k % 2, :] for k in range(4)]
    xht = [sum_p[:, k // 2, k % 2, :] for k in range(4)]

    ps_prod = ps("ps_prod", [P, 2, SUB, C])
    ps_x = ps("ps_x", [P, 2, BW])
    ps_y = ps("ps_y", [P, 2, BW])
    ps_gate = ps_y[:, 0, 0:NT * E].rearrange("p (t e) -> p t e", e=E)

    const_loaded = sem("const_loaded")
    w_loaded = sem("w_loaded")
    gate_loaded = sem("gate_loaded")
    ident = consts[:, at_const["ident"]]
    x_loaded = [sem(f"x_loaded{i}") for i in range(NPAIR)]
    raw_loaded = [sem(f"raw_loaded{i}") for i in range(RING)]
    ones_set = sem("ones_set")
    w_high = sem("w_high")
    w_low = sem("w_low")
    v_step = sem("v_step")
    var_inv = sem("var_inv")
    rstd_ready = sem("rstd_ready")
    var_root = sem("var_root")
    xn_ready = sem("xn_ready")
    xt_made = sem("xt_made")
    xt_high = sem("xt_high")
    xt_low = sem("xt_low")
    y_made = sem("y_made")
    y_high = sem("y_high")
    y_low = sem("y_low")
    summed_a = sem("summed_a")
    halved = sem("halved")
    summed_v = sem("summed_v")
    summed_p = sem("summed_p")
    folded_p = sem("folded_p")
    folded = sem("folded")
    deg_made = sem("deg_made")
    deg_inv = sem("deg_inv")
    deg_root = sem("deg_root")
    dinv_ready = sem("dinv_ready")
    z_high = sem("z_high")
    z_low = sem("z_low")
    z_added = sem("z_added")
    a_high = sem("a_high")
    a_low = sem("a_low")
    block_done = sem("block_done")
    acc_added = sem("acc_added")
    xe_loaded = [sem(f"xe_loaded{i}") for i in range(2)]
    e_ready = sem("e_ready")
    relu_made = sem("relu_made")
    relu_added = sem("relu_added")
    x2_ready = sem("x2_ready")
    var2_inv = sem("var2_inv")
    var2_root = sem("var2_root")
    xh_ready = sem("xh_ready")
    xh_turned = sem("xh_turned")
    xht_ready = sem("xht_ready")
    logits_made = sem("logits_made")
    relu_end_made = sem("relu_end_made")
    relu_end_added = sem("relu_end_added")
    x_end_loaded = sem("x_end_loaded")
    rows_stored = [sem(f"rows_stored{i}") for i in range(4)]
    lg_ready = sem("lg_ready")

    x_pair = x.rearrange("(b t p) c -> b p t c", t=PT, p=P)
    x_v = x.rearrange("(b t p) c -> b p t c", t=YT, p=P)
    rows_v = rows.rearrange("(b t p) c -> b p t c", t=YT, p=P)
    BP = PT // YT

    adj_rows_v = adj_rows.rearrange("(b r p) (jp j) -> b jp p r j", r=2, p=P, jp=NPAIR)

    def rows_added(b):
        return [p.n_prod for p in every if p.kind == PROD and p.t == last_t][0] // 2 + b * YT // SUB + 1

    def n_both(t):
        return sum(b.kind == BOTH for b in every if b.t <= t)

    def n_sums(t):
        return max(b.n_deg + 1 for b in every if b.kind == DEG and b.ip == t)

    block = ctx.enter_context(nc.Block())

    @block.sync
    def _(sp):
        def load_x(t):
            sp.dma_start(acc[:, t * PT:(t + 1) * PT, :], x_pair[t]).then_inc(x_loaded[t], 16)

        def store_rows(pair):
            for q in range(BP):
                b = pair * BP + q
                sp.wait_ge(xh_ready, b + 1)
                sp.dma_start(rows_v[b], xh[q].rearrange("p (t c) -> p t c", t=YT)).then_inc(rows_stored[q], 16)

        load_x(0)
        sp.dma_start(w_raw[:, :, :], w.rearrange("(k p) c -> p k c", p=P)).then_inc(w_loaded, 16)
        sp.dma_start(consts[:, :], const).then_inc(const_loaded, 16)
        for b in every:
            if b.n >= RING:
                old = at[b.n - RING]
                if old.kind == DEG:
                    sp.wait_ge(summed_a, old.n_deg + 1)
                if old.kind == BOTH:
                    sp.wait_ge(summed_v, old.n_both + 1)
                    sp.wait_ge(summed_p, old.n_both + 1)
                if old.multiplies:
                    sp.wait_ge(a_low, old.n_prod + 1)
            if b.kind == DEG:
                sp.dma_start(raw[:, b.slot, :, :].rearrange("p (r a) j -> p r (a j)", r=2),
                             adj_rows_v[b.ip * SUB + b.s, b.jp]).then_inc(raw_loaded[b.slot], 16)
            else:
                sp.dma_start(raw[:, b.slot, :, :], adj[b.j, b.i]).then_inc(raw_loaded[b.slot], 16)
            if b.n in (0, 1, 2):
                load_x(b.n + 1)
            if b.n == RING:
                sp.dma_start(gw[:, :, :], gate_w.rearrange("(k p) e -> p k e", p=P)).then_inc(gate_loaded, 16)
                sp.dma_start(gb[:, 0, :], gate_b.partition_broadcast(P)).then_inc(gate_loaded, 16)
            if b.kind == PROD and b.t == last_t and b.ip >= 2 and b.s == 3:
                store_rows(b.ip - 2)
        sp.wait_ge(a_low, every[-4].n_prod + 1)
        sp.dma_start(x_end.rearrange("p a i -> p (a i)").rearrange("p (t c) -> p t c", c=C), x_pair[last_t]
                     ).then_inc(x_end_loaded, 16)
        store_rows(NPAIR - 2)
        sp.wait_ge(block_done, every[-1].n_prod + 1)
        for n in range(EARLY):
            weights.load(sp, n, early[n])
        store_rows(NPAIR - 1)
        for q in range(4):
            sp.wait_ge(rows_stored[q], 16 * NPAIR)

    @block.gpsimd
    def _(pool):
        pool.memset(ones[:, :], 1.0).then_inc(ones_set, 1)

        def halve(b):
            pool.wait_ge(raw_loaded[b.slot], 16 * b.load)
            halves = raw[:, b.slot, :, :].rearrange("p (r a) j -> p r a j", r=2)
            pool.tensor_tensor(halves[:, :, 0, :], halves[:, :, 0, :], halves[:, :, 1, :], ALU.add
                               ).then_inc(halved, 1)

        def sum_block(b):
            pool.wait_ge(raw_loaded[b.slot], 16 * b.load)
            out = sum_p[:, b.strip, :, :]
            src = raw[:, b.slot, 2:4, :]
            if b.n_both:
                pool.wait_ge(summed_p, b.n_both)
            if b.jp == 0 and b.s % 2 == 0:
                if b.ip > 1:
                    pool.wait_ge(folded, b.ip - 1)
                pool.tensor_copy(out, src).then_inc(summed_p, 1)
            else:
                pool.tensor_tensor(out, out, src, ALU.add).then_inc(summed_p, 1)
            if b.n_both + 1 == n_both(b.t):
                pool.wait_ge(summed_p, b.n_both + 1)
                pool.tensor_tensor(sum_p[:, :, 0, :], sum_p[:, :, 0, :], sum_p[:, :, 1, :], ALU.add
                                   ).then_inc(folded_p, 1)

        for b in every:
            if b.halved:
                halve(b)
            if b.kind == BOTH:
                sum_block(b)

        def load_x(b):
            if b >= 2:
                pool.wait_ge(relu_added, b - 1)
            pool.dma_start(xe[b % 2].rearrange("p (t c) -> p t c", t=YT), x_v[b]).then_inc(xe_loaded[b % 2], 16)

        pool.wait_ge(z_added, NPAIR)
        load_x(0)
        load_x(1)
        for b in range(NY - BP):
            pool.wait_ge(xe_loaded[b % 2], 16 * (b // 2 + 1))
            pool.wait_ge(e_ready, b + 1)
            for n in range(b * YT, (b + 1) * YT):
                last = pool.tensor_scalar(acc[:, n, :], acc[:, n, :], 0.0, dinv[:, n:n + 1], ALU.max, ALU.mult)
            last.then_inc(relu_made, 1)
            pool.wait_ge(relu_made, b + 1)
            a = acc[:, b * YT:(b + 1) * YT, :].rearrange(flat)
            pool.tensor_tensor(a, a, xe[b % 2], ALU.add).then_inc(relu_added, 1)
            if b + 2 < NY - BP:
                load_x(b + 2)
        pool.wait_ge(x_end_loaded, 16)
        for q in range(BP):
            pool.wait_ge(relu_end_made, q + 1)
            b = last_t * BP + q
            a = acc[:, b * YT:(b + 1) * YT, :].rearrange(flat)
            pool.tensor_tensor(a, a, x_end[:, q, :], ALU.add).then_inc(relu_end_added, 1)
        for n in range(EARLY):
            weights.low_part(pool, n, early[n])

    @block.scalar
    def _(act):
        def xt_high_part(b):
            act.wait_ge(xt_made, b + 1)
            if b >= 2:
                act.wait_ge(y_made, b - 1)
            act.activation(xtr[:, b % 2, :], ps_x[:, b % 2, :], ACT.Copy).then_inc(xt_high, 1)

        def y_high_part(b):
            act.wait_ge(y_made, b + 1)
            act.activation(zr[:, b * YT:(b + 1) * YT, :].rearrange(flat), ps_y[:, b % 2, :],
                           ACT.Copy).then_inc(y_high, 1)

        def a_high_part(b):
            act.wait_ge(raw_loaded[b.slot], 16 * b.load)
            if b.n_prod >= 2:
                act.wait_ge(block_done, b.n_prod - 1)
            act.activation(ar[:, b.n_prod % 2, :, :], raw[:, b.slot, :, :], ACT.Copy).then_inc(a_high, 1)

        def sum_rows(b):
            if b.halved:
                act.wait_ge(halved, b.n_deg + 1)
            else:
                act.wait_ge(raw_loaded[b.slot], 16 * b.load)
            for k in range(2):
                tile = b.ip * PT + b.s * 2 + k
                half = raw[:, b.slot, 2 * k:2 * k + (1 if b.halved else 2), :]
                last = act.activation(half, half, ACT.Copy, accum_out=sum_a[:, tile, b.jp:b.jp + 1])
            last.then_inc(summed_a, 1)

        def degree_root(t):
            act.wait_ge(deg_inv, t + 1)
            act.activation(rs[:, 1, :], rs[:, 0, :], ACT.Sqrt).then_inc(deg_root, 1)

        def z_high_part(t):
            act.wait_ge(dinv_ready, t + 1)
            for i in range(PT):
                n = t * PT + i
                last = act.activation(zr[:, n, :], z[:, i, :], ACT.Copy, scale=dinv[:, n:n + 1])
                if i % SUB == SUB - 1:
                    last.then_inc(z_high, 1)

        def exps(b):
            act.wait_ge(acc_added, rows_added(b))
            e, used = (ee[b % 2], b - 1) if b < NY - BP else (ee_end[b % BP], NY - BP)
            if b >= 2:
                act.wait_ge(x2_ready, used)
            for i in range(YT):
                n = b * YT + i
                last = act.activation(e[:, i * C:(i + 1) * C], acc[:, n, :], ACT.Exp, scale=dinv[:, n:n + 1])
            last.then_inc(e_ready, 1)

        def row_root(pair, inv, root):
            act.wait_ge(inv, pair + 1)
            act.activation(rs[:, 1, :], rs[:, 0, :], ACT.Sqrt).then_inc(root, 1)

        def turned_rows(pair, batches):
            for q in batches:
                b = pair * BP + q
                act.wait_ge(xh_turned, b + 1)
                if pair:
                    act.wait_ge(logits_made, b - BP + 1)
                act.activation(xht[q], ps_x[:, q % 2, :], ACT.Copy).then_inc(xht_ready, 1)

        act.wait_ge(w_loaded, 16)
        act.activation(wr[:, :, :], w_raw[:, :, :], ACT.Copy).then_inc(w_high, 1)
        first = list(steps[0][0])
        row_root(0, var_inv, var_root)
        for b in range(1, NY + 2):
            if b % BP == 3 and b // BP + 1 < NPAIR:
                row_root(b // BP + 1, var_inv, var_root)
            if b <= NY:
                xt_high_part(b - 1)
            if b >= 2:
                y_high_part(b - 2)
            if b >= SUM_LAG and first:
                sum_rows(first.pop(0))
        while first:
            sum_rows(first.pop(0))
        for t, (before, after) in enumerate(steps):
            for b in before if t else ():
                if b.kind == DEG:
                    sum_rows(b)
                else:
                    a_high_part(b)
            degree_root(t)
            if t < 2:
                a_high_part(after[0])
            z_high_part(t)
            for b in after[1 if t < 2 else 0:]:
                if b.kind == DEG:
                    sum_rows(b)
                    continue
                pair = b.ip - 1
                last_rows = t == last_t and b.ip
                if last_rows and b.s == 2:
                    exps(pair * BP + 2)
                    exps(pair * BP + 3)
                if last_rows and pair and b.s >= 2:
                    turned_rows(pair - 1, (0, 1) if b.s == 2 else (2, 3))
                a_high_part(b)
                if last_rows and b.s == 0:
                    if pair:
                        row_root(pair - 1, var2_inv, var2_root)
                    exps(pair * BP)
                    exps(pair * BP + 1)
        row_root(last_t - 1, var2_inv, var2_root)
        turned_rows(last_t - 1, range(BP))
        for q in range(BP):
            exps(last_t * BP + q)
        for n in range(EARLY):
            weights.high_part(act, n, early[n])
        row_root(last_t, var2_inv, var2_root)
        turned_rows(last_t, range(BP))

    @block.vector
    def _(dve):
        chain = Chain(dve, v_step)
        step = chain.step

        def newton(out, a, r, tmp, ready=None):
            step(dve.tensor_tensor(tmp, r, r, ALU.mult))
            step(dve.tensor_tensor(tmp, tmp, a, ALU.mult))
            step(dve.tensor_scalar(tmp, tmp, -0.5, 1.5, ALU.mult, ALU.add))
            last = dve.tensor_tensor(out, r, tmp, ALU.mult)
            if ready:
                last.then_inc(ready, 1)
            else:
                step(last)

        def statistics(t, tiles):
            for i in tiles:
                last = dve.bn_stats(stats[:, i, :], acc[:, t * PT + i, :])
            return last

        def variances(t, inv):
            for i in range(PT):
                last = dve.bn_aggr(mv[:, t * PT + i, :], stats[:, i, :])
            step(last)
            step(dve.tensor_scalar(rs[:, 2, :], mv[:, t * PT:(t + 1) * PT, 1], EPS, None, ALU.add))
            dve.reciprocal(rs[:, 0, :], rs[:, 2, :]).then_inc(inv, 1)

        def deviations(t, root):
            dve.wait_ge(root, t + 1)
            newton(rstd[:, t * PT:(t + 1) * PT], rs[:, 2, :], rs[:, 1, :], rs[:, 0, :], rstd_ready)

        def normalise(b):
            dve.wait_ge(rstd_ready, b // BP + 1)
            for i in range(b * YT, (b + 1) * YT):
                last = dve.tensor_scalar(acc[:, i, :], acc[:, i, :], mv[:, i, 0:1], rstd[:, i:i + 1],
                                         ALU.subtract, ALU.mult)
            last.then_inc(xn_ready, 1)

        def xt_low_part(b):
            dve.wait_ge(xt_high, b + 1)
            dve.tensor_tensor(xtl[:, b % 2, :], ps_x[:, b % 2, :], xtr[:, b % 2, :].bitcast(F32),
                              ALU.subtract).then_inc(xt_low, 1)

        def y_low_part(b):
            dve.wait_ge(y_high, b + 1)
            rows_ = slice(b * YT, (b + 1) * YT)
            dve.tensor_tensor(zl[:, rows_, :].rearrange(flat), ps_y[:, b % 2, :],
                              zr[:, rows_, :].rearrange(flat).bitcast(F32), ALU.subtract).then_inc(y_low, 1)

        def sum_block(b):
            dve.wait_ge(raw_loaded[b.slot], 16 * b.load)
            out = sum_v[:, b.strip, :, :]
            src = raw[:, b.slot, 0:2, :]
            if b.n_both:
                dve.wait_ge(summed_v, b.n_both)
            if b.jp == 0 and b.s % 2 == 0:
                if b.t > 1:
                    dve.wait_ge(deg_made, b.t - 1)
                dve.tensor_copy(out, src).then_inc(summed_v, 1)
            else:
                dve.tensor_tensor(out, out, src, ALU.add).then_inc(summed_v, 1)

        def fold(t):
            dve.wait_ge(summed_v, n_both(t))
            step(dve.tensor_tensor(sum_v[:, :, 0, :], sum_v[:, :, 0, :], sum_v[:, :, 1, :], ALU.add))
            dve.wait_ge(folded_p, t)
            dve.tensor_tensor(sum_v[:, :, 0, :], sum_v[:, :, 0, :], sum_p[:, :, 0, :], ALU.add).then_inc(folded, 1)

        pending = []
        strips = [0]

        def add_strip():
            b = pending.pop(0)
            dve.wait_ge(block_done, b.n_prod + 1)
            if strips[0]:
                dve.wait_ge(acc_added, strips[0])
            strips[0] += 1
            out = acc[:, b.i * SUB:(b.i + 1) * SUB, :]
            if b.kind == BOTH and b.jp == 0:
                dve.tensor_copy(out, ps_prod[:, b.strip, :, :]).then_inc(acc_added, 1)
            else:
                dve.tensor_tensor(out, ps_prod[:, b.strip, :, :], out, ALU.add).then_inc(acc_added, 1)

        def a_low_part(b):
            dve.wait_ge(a_high, b.n_prod + 1)
            k = b.n_prod % 2
            dve.tensor_tensor(al[:, k, :, :], raw[:, b.slot, :, :], ar[:, k, :, :].bitcast(F32),
                              ALU.subtract).then_inc(a_low, 1)
            if pending and pending[0].n_prod + 2 <= b.n_prod:
                add_strip()
            if b.s % 2 == 1:
                pending.append(b)

        def z_whole(t):
            pair = slice(t * PT, (t + 1) * PT)
            if t:
                dve.wait_ge(z_added, t)
            step(dve.tensor_tensor(z[:, :, :], zr[:, pair, :].bitcast(F32), zl[:, pair, :].bitcast(F32), ALU.add))

        def degrees(t):
            dve.wait_ge(summed_a, n_sums(t))
            step(dve.tensor_reduce(rs[:, 2, :], sum_a[:, t * PT:(t + 1) * PT, t:], AX.X, ALU.add))
            step(dve.tensor_scalar(rs[:, 2, :], rs[:, 2, :], 1.0, None, ALU.add))
            if t:
                dve.wait_ge(deg_made, t)
                step(dve.tensor_tensor(rs[:, 2, :], rs[:, 2, :], ps_x[:, 0, 0:PT], ALU.add))
            dve.reciprocal(rs[:, 0, :], rs[:, 2, :]).then_inc(deg_inv, 1)
            dve.wait_ge(deg_root, t + 1)
            newton(dinv[:, t * PT:(t + 1) * PT], rs[:, 2, :], rs[:, 1, :], rs[:, 0, :], dinv_ready)

        def z_low_part(t):
            for half in range(2):
                dve.wait_ge(z_high, 2 * t + half + 1)
                for i in range(half * SUB, (half + 1) * SUB):
                    n = t * PT + i
                    last = dve.scalar_tensor_tensor(zl[:, n, :], z[:, i, :], dinv[:, n:n + 1],
                                                    zr[:, n, :].bitcast(F32), ALU.mult, ALU.subtract)
                last.then_inc(z_low, 1)

        def add_z(t):
            if strips[0]:
                dve.wait_ge(acc_added, strips[0])
            for i in range(PT):
                n = t * PT + i
                if t:
                    last = dve.scalar_tensor_tensor(acc[:, n, :], z[:, i, :], dinv[:, n:n + 1], acc[:, n, :],
                                                    ALU.mult, ALU.add)
                else:
                    last = dve.tensor_scalar(acc[:, n, :], z[:, i, :], dinv[:, n:n + 1], None, ALU.mult)
            last.then_inc(z_added, 1)
            dve.wait_ge(z_added, t + 1)

        def x2(b):
            a = acc[:, b * YT:(b + 1) * YT, :].rearrange(flat)
            e = ee[b % 2]
            if b < NY - BP:
                dve.wait_ge(relu_added, b + 1)
            else:
                dve.wait_ge(relu_end_added, b - (NY - BP) + 1)
                e = ee_end[b % BP]
            dve.scalar_tensor_tensor(a, e, 1.0, a, ALU.min, ALU.add).then_inc(x2_ready, 1)

        def relu(b):
            dve.wait_ge(e_ready, b + 1)
            for n in range(b * YT, (b + 1) * YT):
                last = dve.tensor_scalar(acc[:, n, :], acc[:, n, :], 0.0, dinv[:, n:n + 1], ALU.max, ALU.mult)
            last.then_inc(relu_end_made, 1)

        def normalise_rows(pair):
            dve.wait_ge(rstd_ready, NPAIR + pair + 1)
            for q in range(BP):
                b = pair * BP + q
                if pair:
                    dve.wait_ge(rows_stored[q], 16 * pair)
                    dve.wait_ge(xh_turned, b - BP + 1)
                for i in range(YT):
                    n = b * YT + i
                    last = dve.tensor_scalar(xh[q][:, i * C:(i + 1) * C], acc[:, n, :], mv[:, n, 0:1],
                                             rstd[:, n:n + 1], ALU.subtract, ALU.mult)
                last.then_inc(xh_ready, 1)

        def variances2(pair):
            dve.wait_ge(x2_ready, (pair + 1) * BP)
            step(statistics(pair, range(PT)))
            variances(pair, var2_inv)

        dve.wait_ge(w_high, 1)
        dve.tensor_tensor(wl[:, :, :], w_raw[:, :, :], wr[:, :, :].bitcast(F32), ALU.subtract).then_inc(w_low, 1)
        dve.wait_ge(x_loaded[0], 16)
        step(statistics(0, range(PT)))
        variances(0, var_inv)
        deviations(0, var_root)
        normalise(0)

        def prepare(b):
            pair, phase = b // BP + 1, b % BP
            if pair == NPAIR or b >= NY:
                return
            if phase == 0:
                dve.wait_ge(x_loaded[pair], 16)
            if phase < 3:
                last = statistics(pair, range(3 * phase, min(3 * phase + 3, PT)))
            if phase == 2:
                step(last)
                variances(pair, var_inv)
            if phase == 3:
                deviations(pair, var_root)

        prepare(0)
        for b in range(1, NY + 2):
            if b < NY:
                normalise(b)
            if b <= NY:
                xt_low_part(b - 1)
            if b >= 2:
                y_low_part(b - 2)
            prepare(b)
        for t, (before, after) in enumerate(steps):
            z_whole(t)
            if t:
                both = [b for b in before if b.multiplies]
                for b in both[:-2]:
                    sum_block(b)
                    a_low_part(b)
                if before[-1].multiplies:
                    sum_block(both[-2])
                    sum_block(both[-1])
                    fold(t)
                    for b in both[-2:]:
                        a_low_part(b)
                else:
                    for b in both[-2:]:
                        sum_block(b)
                        a_low_part(b)
                    fold(t)
            degrees(t)
            if t < 2:
                a_low_part(after[0])
            z_low_part(t)
            for b in after:
                if b.kind == DEG:
                    continue
                pair = b.ip - 1
                if t >= 2 or b is not after[0]:
                    a_low_part(b)
                if b.ip == 0 and b.s == 1:
                    add_z(t)
                if t == last_t and b.ip:
                    if b.s == 0 and pair:
                        deviations(pair - 1, var2_root)
                        normalise_rows(pair - 1)
                    x2(pair * BP + b.s)
                    if b.s == 3:
                        variances2(pair)
        deviations(last_t - 1, var2_root)
        normalise_rows(last_t - 1)
        while pending:
            add_strip()
        for q in range(BP):
            relu(last_t * BP + q)
        for q in range(BP + 1):
            if q < BP:
                x2(last_t * BP + q)
            if q:
                dve.wait_ge(x2_ready, last_t * BP + q)
                last = statistics(last_t, range((q - 1) * YT, q * YT))
        step(last)
        variances(last_t, var2_inv)
        deviations(last_t, var2_root)
        normalise_rows(last_t)
        dve.wait_ge(logits_made, NY)
        dve.wait_ge(gate_loaded, 32)
        dve.tensor_tensor(lg[:, :, :], ps_gate, gb[:, :, :].broadcast_to([P, NT, E]), ALU.add).then_inc(lg_ready, 1)
        dve.wait_ge(lg_ready, 1)

    @block.tensor
    def _(pe):
        def transposes(b):
            pe.wait_ge(xn_ready, b + 1)
            if b >= 2:
                pe.wait_ge(xt_low, b - 1)
            for i in range(YT):
                for k in range(KC):
                    at_ = (i * KC + k) * P
                    last = pe.transpose(ps_x[:, b % 2, at_:at_ + P], acc[:, b * YT + i, k * P:(k + 1) * P], ident)
            last.then_inc(xt_made, 1)

        def y_tiles(b):
            pe.wait_ge(xt_low, b + 1)
            if b >= 2:
                pe.wait_ge(y_low, b - 1)
            for i in range(YT):
                for k in range(KC):
                    at_ = (i * KC + k) * P
                    hi, lo = (v[:, b % 2, at_:at_ + P] for v in (xtr, xtl))
                    for q, (lhs, rhs) in enumerate(((hi, wr), (hi, wl), (lo, wr))):
                        last = pe.matmul(ps_y[:, b % 2, i * C:(i + 1) * C], lhs, rhs[:, k, :],
                                         start=(i == 0 and k == 0 and q == 0), stop=(k == KC - 1 and q == 2),
                                         skip_group_check=True)
            last.then_inc(y_made, 1)

        def product_group(first, added, j_tile, between=None):
            for s in range(4):
                strip, half = s // 2, s % 2
                pe.wait_ge(a_low, first + (s + 1))
                if half == 0 and added is not None:
                    pe.wait_ge(acc_added, added + strip)
                for i in range(SUB):
                    for sub in range(SUB):
                        hi, lo = (v[:, s % 2, sub, i * P:(i + 1) * P] for v in (ar, al))
                        tile = j_tile + (half * SUB + sub)
                        mh, ml = (v[:, bass.ds(tile, 1), :].rearrange(flat) for v in (zr, zl))
                        for q, (lhs, rhs) in enumerate(((hi, mh), (hi, ml), (lo, mh))):
                            last = pe.matmul(ps_prod[:, strip, i, :], lhs, rhs,
                                             start=(half == 0 and i % 2 == 0 and sub == 0 and q == 0),
                                             stop=(half == 1 and sub == SUB - 1 and q == 2),
                                             skip_group_check=True)
                last.then_inc(block_done, 1)
                if between and s < 3:
                    between(s)

        def degrees(t):
            pe.wait_ge(folded, t)
            for i in range(PT):
                part = sum_v[:, i // SUB, 0, i % SUB * P:(i % SUB + 1) * P]
                last = pe.matmul(ps_x[:, 0, i:i + 1], part, ones[:, :], start=True, stop=True)
            last.then_inc(deg_made, 1)

        def turn_rows(first, batches):
            for q in batches:
                pe.wait_ge(xh_ready, first + (q + 1))
                if q >= 2:
                    pe.wait_ge(xht_ready, first + (q - 1))
                for m in range(YT * KC):
                    last = pe.transpose(ps_x[:, q % 2, m * P:(m + 1) * P], xh[q][:, m * P:(m + 1) * P], ident)
                last.then_inc(xh_turned, 1)

        def row_logits(first, batches):
            for q in batches:
                pe.wait_ge(xht_ready, first + (q + 1))
                for i in range(YT):
                    out = ps_y[:, 0, bass.ds((first + q) * (YT * E) + i * E, E)]
                    for k in range(KC):
                        m = i * KC + k
                        last = pe.matmul(out, xht[q][:, m * P:(m + 1) * P], gw[:, k, :],
                                         start=(k == 0), stop=(k == KC - 1), skip_group_check=True)
                last.then_inc(logits_made, 1)

        def logits_step(first, s):
            if s:
                row_logits(first, (2 * s - 2, 2 * s - 1))
            if s < 2:
                turn_rows(first, (2 * s, 2 * s + 1))

        pe.wait_ge(w_low, 1)
        pe.wait_ge(ones_set, 1)
        pe.wait_ge(const_loaded, 16)
        for b in range(NY + 1):
            if b < NY:
                transposes(b)
            if b:
                y_tiles(b - 1)
        pe.wait_ge(y_low, NY)
        for t, (before, after) in enumerate(steps):
            lower = [b for b in before if b.multiplies]
            if t >= 2:
                base = lower[0].n_prod
                with pe.Fori(0, t - 1) as g:
                    product_group(g * 4 + base, g * 2 + (base // 2 - 1), g * PT)
            if t:
                base = lower[-4].n_prod
                inside = before[-1].multiplies
                product_group(base, base // 2 - 1, (t - 1) * PT,
                              lambda s: degrees(t) if s == 1 and inside else None)
                if not inside:
                    degrees(t)
            base = [b for b in after if b.multiplies][0].n_prod
            pe.wait_ge(z_low, 2 * t + 1)
            product_group(base, base // 2 - 1 if t else None, t * PT,
                          lambda s: pe.wait_ge(z_low, 2 * t + 2) if s == 0 else None)
            if 0 < t < last_t:
                with pe.Fori(0, t) as g:
                    product_group(g * 4 + (base + 4), g * 2 + (base // 2 + 1), t * PT)
            if t == last_t:
                pe.wait_ge(gate_loaded, 32)
                product_group(base + 4, base // 2 + 1, t * PT)
                with pe.Fori(0, t - 1) as g:
                    product_group(g * 4 + (base + 8), g * 2 + (base // 2 + 3), t * PT,
                                  lambda s: logits_step(g * BP, s))
                for pair in (last_t - 1, last_t):
                    for s in range(3):
                        logits_step(pair * BP, s)


class Weights:

    COUNT = 2 * E

    def __init__(self, nc, ctx, w1, w2):
        self.nc, self.ctx, self.w1, self.w2 = nc, ctx, w1, w2
        self.w1r, self.w1l = self.tensor("w1r", KC, F), self.tensor("w1l", KC, F)
        self.w2r, self.w2l = None, self.tensor("w2l", KF, C)
        self.loaded = [ctx.enter_context(nc.semaphore(f"weights_loaded{n}")) for n in range(self.COUNT)]
        self.high_ready = ctx.enter_context(nc.semaphore("weights_high_ready"))
        self.low_ready = ctx.enter_context(nc.semaphore("weights_low_ready"))

    def tensor(self, name, chunks, width):
        return self.ctx.enter_context(self.nc.sbuf_tensor(name, [P, E, chunks, width], F32R))

    def parts(self, n):
        high, low = (self.w1r, self.w1l) if n < E else (self.w2r, self.w2l)
        return high[:, n % E].rearrange("p k f -> p (k f)"), low[:, n % E].rearrange("p k f -> p (k f)")

    def load(self, sp, n, buffer):
        src = self.w1[n] if n < E else self.w2[n - E]
        sp.dma_start(buffer.rearrange("p (k f) -> p k f", f=src.shape[1]), src.rearrange("(k p) f -> p k f", p=P)
                     ).then_inc(self.loaded[n], 16)

    def high_part(self, act, n, buffer):
        act.wait_ge(self.loaded[n], 16)
        act.activation(self.parts(n)[0], buffer, ACT.Copy).then_inc(self.high_ready, 1)

    def low_part(self, pool, n, buffer):
        high, low = self.parts(n)
        pool.wait_ge(self.high_ready, n + 1)
        pool.tensor_tensor(low, buffer, high.bitcast(F32), ALU.subtract).then_inc(self.low_ready, 1)


def route(nc, ctx, weights, b1, consts, at, lg, wts, ids, dst, tile_expert, b1a, b1_loaded):

    def sb(name, shape, dt=F32):
        return ctx.enter_context(nc.sbuf_tensor(name, shape, dt))

    def ps(name, shape):
        return ctx.enter_context(nc.psum_tensor(name, shape, F32))

    def sem(name):
        return ctx.enter_context(nc.semaphore(name))

    STAGES = 4
    stage = [b1a[:, 2 * k:2 * k + 2, :].rearrange("p e f -> p (e f)") for k in range(STAGES)]
    GROUP = 8

    ps_cnt = ps("ps_cnt", [P, NT, E])
    ps_tot = ps("ps_tot", [P, NT, E])
    ps_ids = ps("ps_ids", [P, 2, SLOTS])

    v_chain = sem("v_chain2")
    equal_ready = sem("equal_ready")
    row_ready = sem("row_ready")
    diff_ready = sem("diff_ready")
    exp_ready = sem("exp_ready")
    mask_ready = sem("mask_ready")
    counts_ready = sem("counts_ready")
    hot_ready = sem("hot_ready")
    hot_used = sem("hot_used")

    l2 = sb("l2", [P, NT, E])
    cand = sb("cand", [P, NT, E])
    hot1 = sb("hot1", [P, NT, E])
    hot2 = sb("hot2", [P, NT, E])
    mask = sb("mask", [P, NT, E])
    col = sb("col", [P, 8, NT])
    tot = sb("tot", [P, E, NT])
    keep = sb("keep", [P, E, NT])
    incl = sb("incl", [P, E, NT])
    ex = sb("ex", [P, 6, E])
    ti = sb("ti", [P, SLOTS, E])
    tf = sb("tf", [P, SLOTS])
    pos = sb("pos", [P, CW])
    pos_i = sb("pos_i", [P, 2, CW], I32)
    pos_f = sb("pos_f", [P, 2, CW])
    pos_b = sb("pos_b", [P, 2, CW], BF16)
    hot_r = sb("hot_r", [P, 2, GROUP, P], BF16)
    equal = sb("equal", [P, 2, GROUP, SLOTS], BF16)
    hot_q = sb("hot_q", [P, 2, GROUP, 2, SLOTS], BF16)
    ones = sb("ones2", [P, P])
    lane_b = sb("lane_b", [P, P], BF16)
    tile_b = sb("tile_b", [P, SLOTS], BF16)
    column_b = sb("column_b", [P, CW], BF16)
    v = incl[:, :, :].rearrange("p e t -> p (e t)")[:, 0:SLOTS]
    pad = tot[:, :, :].rearrange("p e t -> p (e t)")[:, 0:SLOTS]
    ones2_set = sem("ones2_set")

    def K(name):
        return consts[:, at[name]]

    block = ctx.enter_context(nc.Block())

    @block.gpsimd
    def _(pool):
        pool.memset(ones[:, :], 1.0).then_inc(ones2_set, 1)
        pool.memset(keep[:, :, :], 1.0).then_inc(ones2_set, 1)
        pool.wait_ge(ones2_set, 2)
        pool.memset(keep[:, :, 0:1], 0.0).then_inc(ones2_set, 1)
        for n in range(EARLY, Weights.COUNT):
            weights.low_part(pool, n, stage[n % STAGES])

    @block.sync
    def _(sp):
        for n in range(EARLY, Weights.COUNT):
            if n >= EARLY + STAGES:
                sp.wait_ge(weights.low_ready, n - STAGES + 1)
            weights.load(sp, n, stage[n % STAGES])
        sp.wait_ge(weights.low_ready, Weights.COUNT)
        sp.dma_start(b1a[:, :, :], b1.rearrange("e f -> (e f)").partition_broadcast(P)).then_inc(b1_loaded, 16)

    @block.scalar
    def _(act):
        matrices = list(range(EARLY, Weights.COUNT))
        for n in matrices[:2]:
            weights.high_part(act, matrices.pop(0), stage[n % STAGES])
        act.wait_ge(diff_ready, 1)
        act.activation(col[:, 3, :], col[:, 2, :], ACT.Exp).then_inc(exp_ready, 1)
        for g in range(CW // GROUP):
            for n in matrices[:2 if g == 0 else 1]:
                weights.high_part(act, matrices.pop(0), stage[n % STAGES])
            act.wait_ge(equal_ready, g + 1)
            if g >= 2:
                act.wait_ge(hot_used, g - 1)
            act.activation(hot_q[:, g % 2, :, 1, :], equal[:, g % 2], ACT.Copy, scale=K("row")
                           ).then_inc(row_ready, 1)
        for n in matrices:
            weights.high_part(act, n, stage[n % STAGES])

    @block.vector
    def _(dve):
        ch = Chain(dve, v_chain)
        step = ch.step

        def over_e(ap):
            return ap.unsqueeze(2).broadcast_to([P, NT, E])

        def over_t(ap):
            return ap.unsqueeze(1).broadcast_to([P, NT, E])

        dve.tensor_copy(lane_b[:, :], K("lane"))
        dve.tensor_copy(column_b[:, :], K("column"))
        step(dve.tensor_copy(tile_b[:, :], K("tile")))
        idx = over_t(K("expert"))

        def pick(src, top, hot):
            step(dve.tensor_reduce(top, src, AX.X, ALU.max))
            step(dve.tensor_tensor(cand[:, :, :], src, over_e(top), ALU.is_equal))
            step(dve.scalar_tensor_tensor(cand[:, :, :], cand[:, :, :], -float(E), idx, ALU.mult, ALU.add))
            step(dve.tensor_reduce(col[:, 7, :], cand[:, :, :], AX.X, ALU.min))
            step(dve.tensor_tensor(hot, cand[:, :, :], over_e(col[:, 7, :]), ALU.is_equal))

        pick(lg[:, :, :], col[:, 0, :], hot1[:, :, :])
        step(dve.scalar_tensor_tensor(l2[:, :, :], hot1[:, :, :], -FAR, lg[:, :, :], ALU.mult, ALU.add))
        pick(l2[:, :, :], col[:, 1, :], hot2[:, :, :])
        dve.tensor_tensor(col[:, 2, :], col[:, 1, :], col[:, 0, :], ALU.subtract).then_inc(diff_ready, 1)
        dve.tensor_tensor(mask[:, :, :], hot1[:, :, :], hot2[:, :, :], ALU.add).then_inc(mask_ready, 1)
        dve.wait_ge(exp_ready, 1)
        step(dve.tensor_scalar(col[:, 4, :], col[:, 3, :], 1.0, None, ALU.add))
        step(dve.reciprocal(wts[:, 0, :], col[:, 4, :]))
        step(dve.tensor_tensor(wts[:, 1, :], wts[:, 0, :], col[:, 3, :], ALU.mult))
        dve.wait_ge(counts_ready, 1)
        dve.wait_ge(ones2_set, 3)
        step(dve.tensor_copy(tot[:, :, :], ps_tot[:, :, :].rearrange("p t e -> p e t")))
        step(dve.tensor_tensor_scan(incl[:, :, :].rearrange("p e t -> p (e t)"),
                                    keep[:, :, :].rearrange("p e t -> p (e t)"),
                                    tot[:, :, :].rearrange("p e t -> p (e t)"), 0.0, ALU.mult, ALU.add))
        rows_e = incl[:, :, NT - 1:NT].broadcast_to([P, E, NT])
        full = cand[:, :, :].rearrange("p t e -> p (t e)").rearrange("p (e t) -> p e t", e=E)
        step(dve.tensor_tensor(full, rows_e, K("step").unsqueeze(1).broadcast_to([P, E, NT]), ALU.is_gt))
        step(dve.tensor_reduce(ex[:, 0, :], full, AX.X, ALU.add))
        step(dve.tensor_tensor_scan(ex[:, 1, :], ones[:, 0:E], ex[:, 0, :], 0.0, ALU.mult, ALU.add))
        step(dve.tensor_tensor(ex[:, 2, :], ex[:, 1, :], ex[:, 0, :], ALU.subtract))
        step(dve.tensor_scalar(ex[:, 3, :], ex[:, 2, :], float(P), None, ALU.mult))
        step(dve.tensor_tensor(incl[:, :, :], incl[:, :, :], tot[:, :, :], ALU.subtract))
        step(dve.tensor_tensor(incl[:, :, :], incl[:, :, :], ex[:, 3, :].unsqueeze(2).broadcast_to([P, E, NT]),
                               ALU.add))
        step(dve.tensor_tensor(l2[:, :, :], ps_cnt[:, :, :], incl[:, :, :].rearrange("p e t -> p t e"), ALU.add))
        for k, hot in enumerate((hot1, hot2)):
            step(dve.tensor_tensor(cand[:, :, :], hot[:, :, :], l2[:, :, :], ALU.mult))
            step(dve.tensor_reduce(pos[:, k * NT:(k + 1) * NT], cand[:, :, :], AX.X, ALU.add))
        step(dve.tensor_copy(pos_i[:, 0, :], pos[:, :]))
        step(dve.tensor_scalar(pos_i[:, 1, :], pos_i[:, 0, :], P - 1, None, ALU.bitwise_and))
        step(dve.tensor_copy(pos_f[:, 1, :], pos_i[:, 1, :]))
        step(dve.tensor_tensor(pos_f[:, 0, :], pos[:, :], pos_f[:, 1, :], ALU.subtract))
        step(dve.tensor_scalar(pos_f[:, 0, :], pos_f[:, 0, :], 1.0 / P, None, ALU.mult))
        step(dve.tensor_copy(pos_b[:, :, :], pos_f[:, :, :]))

        def hots(g):
            k, columns = g % 2, slice(g * GROUP, (g + 1) * GROUP)

            def spread_over(ap, width):
                return ap[:, columns].unsqueeze(2).broadcast_to([P, GROUP, width])

            if g >= 2:
                dve.wait_ge(row_ready, g - 1)
                dve.wait_ge(hot_used, g - 1)
            dve.tensor_tensor(equal[:, k], tile_b[:, :].unsqueeze(1).broadcast_to([P, GROUP, SLOTS]),
                              spread_over(pos_b[:, 0, :], SLOTS), ALU.is_equal).then_inc(equal_ready, 1)
            dve.tensor_tensor(hot_r[:, k], lane_b[:, :].unsqueeze(1).broadcast_to([P, GROUP, P]),
                              spread_over(pos_b[:, 1, :], P), ALU.is_equal)
            dve.wait_ge(equal_ready, g + 1)
            dve.tensor_tensor(hot_q[:, k, :, 0, :], equal[:, k], spread_over(column_b, SLOTS), ALU.mult
                              ).then_inc(hot_ready, 1)

        for g in range(CW // GROUP):
            hots(g)
        step(dve.tensor_tensor(ti[:, :, :], ex[:, 1:2, :].broadcast_to([P, SLOTS, E]),
                               K("tile").unsqueeze(2).broadcast_to([P, SLOTS, E]), ALU.is_le))
        step(dve.tensor_reduce(tf[:, :], ti[:, :, :], AX.X, ALU.add))
        step(dve.tensor_scalar(tile_expert[:, :], tf[:, :], float(E - 1), None, ALU.min))
        dve.wait_ge(hot_used, CW // GROUP)
        step(dve.tensor_scalar(v[:, :], ps_ids[:, 0, :], float(P), -float(P), ALU.mult, ALU.add))
        step(dve.tensor_tensor(v[:, :], v[:, :], ps_ids[:, 1, :], ALU.add))
        step(dve.tensor_scalar(pad[:, :], v[:, :], 0.0, None, ALU.is_lt))
        step(dve.tensor_scalar(tf[:, :], K("row").broadcast_to([P, SLOTS]), float(PAD_ROW + P), None, ALU.add))
        step(dve.tensor_tensor(tf[:, :], tf[:, :], pad[:, :], ALU.mult))
        step(dve.tensor_tensor(dst[:, :], tf[:, :], v[:, :], ALU.add))
        step(dve.tensor_scalar(tf[:, :], v[:, :], float(N), -float(N), ALU.is_ge, ALU.mult))
        step(dve.tensor_scalar(v[:, :], v[:, :], 0.0, None, ALU.max))
        step(dve.tensor_tensor(ids[:, :], tf[:, :], v[:, :], ALU.add))

    @block.tensor
    def _(pe):
        pe.wait_ge(mask_ready, 1)
        pe.wait_ge(ones2_set, 1)
        flat = mask[:, :, :].rearrange("p t e -> p (t e)")
        pe.matmul(ps_cnt[:, :, :].rearrange("p t e -> p (t e)"), K("before"), flat, start=True, stop=True)
        pe.matmul(ps_tot[:, :, :].rearrange("p t e -> p (t e)"), ones[:, :], flat, start=True,
                  stop=True).then_inc(counts_ready, 1)

        for g in range(CW // GROUP):
            pe.wait_ge(hot_ready, g + 1)
            pe.wait_ge(row_ready, g + 1)
            for c in range(GROUP):
                last = pe.matmul(ps_ids[:, :, :].rearrange("p h q -> p (h q)"), hot_r[:, g % 2, c, :],
                                 hot_q[:, g % 2, c].rearrange("p h q -> p (h q)"), start=(g == 0 and c == 0),
                                 stop=(g == CW // GROUP - 1 and c == GROUP - 1), skip_group_check=True)
            last.then_inc(hot_used, 1)


class TileExperts:

    def __init__(self, eng, table, first, end):
        self.eng, self.table, self.first, self.end, self.known = eng, table, first, end, {}

    def around(self, n, q):
        self.n, self.q = n, q
        return self

    def of(self, step):
        n = self.n + step
        if n not in self.known:
            self.known[n] = self.eng.value_load(self.table[0:1, bass.ds(self.q + step, 1)], min_val=0,
                                                max_val=E - 1)
        return self.known[n]

    def ahead(self):
        if self.first <= self.n + 1 < self.end:
            self.of(1)


def experts(nc, ctx, b1a, b1_loaded, b2, rows, parts, consts, at, ids, dst, tile_expert, weights):

    def sb(name, shape, dt=F32):
        return ctx.enter_context(nc.sbuf_tensor(name, shape, dt))

    def ps(name, shape):
        return ctx.enter_context(nc.psum_tensor(name, shape, F32))

    def sem(name):
        return ctx.enter_context(nc.semaphore(name))

    UNROLL = 16
    RG = 4
    b2a = sb("b2a", [P, E, C])
    xg = sb("xg", [P, RG, C])
    xgr = sb("xgr", [P, C], F32R)
    xgl = sb("xgl", [P, C], F32R)
    h = sb("h", [P, F])
    hr = sb("hr", [P, 2, F], F32R)
    hl = sb("hl", [P, 2, F], F32R)
    yo = sb("yo", [P, 2, C])

    ps_h = ps("ps_h", [P, 2, F])
    ps_xt = ps("ps_xt", [P, 1, BW])
    ps_ht = ps("ps_ht", [P, 2, F])
    ps_o = ps("ps_o", [P, 2, BW])

    xg_loaded = [sem(f"xg_loaded{i}") for i in range(RG)]
    yo_stored = [sem(f"yo_stored{i}") for i in range(2)]
    b2_loaded = sem("b2_loaded")
    xg_turned = sem("xg_turned")
    xg_high = sem("xg_high")
    xg_low = sem("xg_low")
    h_made = sem("h_made")
    h_ready = sem("h_ready")
    h_turned = sem("h_turned")
    h_high = sem("h_high")
    h_low = sem("h_low")
    o_made = sem("o_made")
    o_ready = sem("o_ready")

    block = ctx.enter_context(nc.Block())

    def is_int(q):
        return isinstance(q, int)

    def stages(eng, stage):
        bodies = (SLOTS - 4) // UNROLL
        first = 3 + UNROLL * bodies
        known = TileExperts(eng, tile_expert, 0, 3)
        for q in range(-1, 3):
            stage(q, q % 4, known.around(q, q))
        with eng.Fori(0, bodies) as i:
            known = TileExperts(eng, tile_expert, 0, UNROLL)
            for n in range(UNROLL):
                stage(i * UNROLL + (n + 3), (n + 3) % 4, known.around(n, i * UNROLL + (n + 3)))
        known = TileExperts(eng, tile_expert, first, SLOTS)
        for q in range(first, SLOTS + 1):
            stage(q, q % 4, known.around(q, q))

    @block.sync
    def _(sp):
        sp.wait_ge(xg_loaded[0], 16)
        sp.dma_start(b2a[:, :, :], b2.rearrange("e f -> (e f)").partition_broadcast(P)).then_inc(b2_loaded, 16)

    @block.gpsimd
    def _(pool):
        def gather(q):
            if q >= RG:
                pool.wait_ge(xg_turned, q - RG + 1)
            pool.indirect_dma_start(xg[:, q % RG, :], None, rows,
                                    bass.IndirectOffsetOnAxis(ap=ids[:, q:q + 1].bitcast(U32), axis=0)
                                    ).then_inc(xg_loaded[q % RG], 16)

        def scatter(q):
            pool.wait_ge(o_ready, q + 1)
            if q >= 1:
                pool.wait_ge(yo_stored[1 - q % 2], 16 * ((q + 1) // 2))
            pool.indirect_dma_start(parts,
                                    bass.IndirectOffsetOnAxis(ap=dst[:, q:q + 1].bitcast(U32), axis=0),
                                    yo[:, q % 2, :], None).then_inc(yo_stored[q % 2], 16)

        for q in range(RG):
            gather(q)
        for q in range(SLOTS):
            scatter(q)
            if q + RG < SLOTS:
                gather(q + RG)
        pool.wait_ge(yo_stored[0], 16 * ((SLOTS + 1) // 2))
        pool.wait_ge(yo_stored[1], 16 * (SLOTS // 2))

    @block.scalar
    def _(act):
        def stage(q, k4, known):
            k = k4 % 2
            if not is_int(q) or q + 1 < SLOTS:
                act.wait_ge(xg_turned, q + 2)
                if not is_int(q) or q >= 0:
                    act.wait_ge(h_made, q + 1)
                act.activation(xgr[:, :], ps_xt[:, 0, 0:C], ACT.Copy).then_inc(xg_high, 1)
            if not is_int(q) or 0 <= q < SLOTS:
                act.wait_ge(h_turned, q + 1)
                if not is_int(q) or q >= 2:
                    act.wait_ge(o_made, q - 1)
                act.activation(hr[:, k, :], ps_ht[:, k, :], ACT.Relu).then_inc(h_high, 1)

        stages(act, stage)

    @block.vector
    def _(dve):
        def stage(q, k4, known):
            k = k4 % 2
            if not is_int(q) or 0 <= q < SLOTS:
                e = known.of(0)
                dve.wait_ge(h_made, q + 1)
                if is_int(q) and q == 0:
                    dve.wait_ge(b1_loaded, 16)
                if not is_int(q) or q >= 1:
                    dve.wait_ge(h_turned, q)
                dve.tensor_tensor(h[:, :], ps_h[:, k, :], b1a[:, bass.ds(e, 1), :].rearrange("p e f -> p (e f)"),
                                  ALU.add).then_inc(h_ready, 1)
            if not is_int(q) or q + 1 < SLOTS:
                dve.wait_ge(xg_high, q + 2)
                dve.tensor_tensor(xgl[:, :], ps_xt[:, 0, 0:C], xgr[:, :].bitcast(F32),
                                  ALU.subtract).then_inc(xg_low, 1)
            known.ahead()
            if not is_int(q) or q >= 1:
                e = known.of(-1)
                dve.wait_ge(o_made, q)
                if is_int(q) and q == 1:
                    dve.wait_ge(b2_loaded, 16)
                if not is_int(q) or q >= 3:
                    dve.wait_ge(yo_stored[1 - k], q * 8 - (8 if k else 16))
                dve.tensor_tensor(yo[:, 1 - k, :], ps_o[:, 1 - k, 0:C],
                                  b2a[:, bass.ds(e, 1), :].rearrange("p e f -> p (e f)"),
                                  ALU.add).then_inc(o_ready, 1)
            if not is_int(q) or 0 <= q < SLOTS:
                dve.wait_ge(h_high, q + 1)
                dve.scalar_tensor_tensor(hl[:, k, :], ps_ht[:, k, :], 0.0, hr[:, k, :].bitcast(F32),
                                         ALU.max, ALU.subtract).then_inc(h_low, 1)

        stages(dve, stage)

    @block.tensor
    def _(pe):
        ident = consts[:, at["ident"]]

        def stage(q, k4, known):
            k = k4 % 2
            if not is_int(q) or 0 <= q < SLOTS:
                e = known.of(0)
                pe.wait_ge(xg_low, q + 1)
                if not is_int(q) or q >= 2:
                    pe.wait_ge(h_ready, q - 1)
                for c in range(KC):
                    hi, lo = xgr[:, c * P:(c + 1) * P], xgl[:, c * P:(c + 1) * P]
                    mh, ml = (v[:, bass.ds(e, 1), c, :].rearrange("p e f -> p (e f)")
                              for v in (weights.w1r, weights.w1l))
                    for n, (lhs, rhs) in enumerate(((hi, mh), (hi, ml), (lo, mh))):
                        last = pe.matmul(ps_h[:, k, :], lhs, rhs, start=(c == 0 and n == 0),
                                         stop=(c == KC - 1 and n == 2))
                last.then_inc(h_made, 1)
            known.ahead()
            if not is_int(q) or q + 1 < SLOTS:
                n = q + 1
                g = (k4 + 1) % RG
                pe.wait_ge(xg_loaded[g], n * 4 + (16 - 4 * g))
                if not is_int(q) or q >= 0:
                    pe.wait_ge(xg_low, n)
                for c in range(KC):
                    last = pe.transpose(ps_xt[:, 0, c * P:(c + 1) * P], xg[:, g, c * P:(c + 1) * P], ident)
                last.then_inc(xg_turned, 1)
            if not is_int(q) or q >= 1:
                e = known.of(-1)
                pe.wait_ge(h_low, q)
                if not is_int(q) or q >= 3:
                    pe.wait_ge(o_ready, q - 2)
                for c in range(KF):
                    hi, lo = hr[:, 1 - k, c * P:(c + 1) * P], hl[:, 1 - k, c * P:(c + 1) * P]
                    mh, ml = (v[:, bass.ds(e, 1), c, :].rearrange("p e f -> p (e f)")
                              for v in (weights.w2r, weights.w2l))
                    for n, (lhs, rhs) in enumerate(((hi, mh), (hi, ml), (lo, mh))):
                        last = pe.matmul(ps_o[:, 1 - k, 0:C], lhs, rhs, start=(c == 0 and n == 0),
                                         stop=(c == KF - 1 and n == 2))
                last.then_inc(o_made, 1)
            if not is_int(q) or 0 <= q < SLOTS:
                pe.wait_ge(h_ready, q + 1)
                if not is_int(q) or q >= 2:
                    pe.wait_ge(h_low, q - 1)
                for c in range(KF):
                    last = pe.transpose(ps_ht[:, k, c * P:(c + 1) * P], h[:, c * P:(c + 1) * P], ident)
                last.then_inc(h_turned, 1)

        stages(pe, stage)


def combine(nc, ctx, parts, out, acc, wts):

    def sem(name):
        return ctx.enter_context(nc.semaphore(name))

    CT = 2
    NBATCH = NT // CT
    y = ctx.enter_context(nc.sbuf_tensor("y", [P, 2, NT, C], F32))
    y_loaded = [sem(f"y_loaded{b}") for b in range(NBATCH)]
    second = sem("second")
    first_added = sem("first_added")
    out_ready = sem("out_ready")
    out_stored = sem("out_stored")
    parts_v = parts[0:2 * N, :].rearrange("(k b t p) c -> k b p t c", k=2, t=CT, p=P)
    out_v = out.rearrange("(b t p) c -> b p t c", t=CT, p=P)

    def batch(b):
        return slice(b * CT, (b + 1) * CT)

    def store(act, b):
        act.wait_ge(out_ready, b + 1)
        act.dma_start(out_v[b], acc[:, batch(b), :]).then_inc(out_stored, 16)

    block = ctx.enter_context(nc.Block())

    @block.sync
    def _(sp):
        for b in range(NBATCH):
            for k in range(2):
                sp.dma_start(y[:, k, batch(b), :], parts_v[k, b]).then_inc(y_loaded[b], 16)

    @block.scalar
    def _(act):
        for b in range(NBATCH):
            act.wait_ge(y_loaded[b], 32)
            for t in range(b * CT, (b + 1) * CT):
                last = act.activation(y[:, 1, t, :], y[:, 1, t, :], ACT.Copy, bias=-1.0, scale=wts[:, 1, t:t + 1])
            last.then_inc(second, 1)
            if b:
                store(act, b - 1)
        store(act, NBATCH - 1)
        act.wait_ge(out_stored, 16 * NBATCH)

    @block.vector
    def _(dve):
        for b in range(NBATCH):
            dve.wait_ge(y_loaded[b], 32)
            for t in range(b * CT, (b + 1) * CT):
                last = dve.scalar_tensor_tensor(acc[:, t, :], y[:, 0, t, :], wts[:, 0, t:t + 1], acc[:, t, :],
                                                ALU.mult, ALU.add)
            last.then_inc(first_added, 1)
            dve.wait_ge(first_added, b + 1)
            dve.wait_ge(second, b + 1)
            dve.tensor_tensor(acc[:, batch(b), :], acc[:, batch(b), :], y[:, 1, batch(b), :],
                              ALU.add).then_inc(out_ready, 1)


def graph_then_experts(nc, x, adj, adj_rows, w, gate_w, gate_b, w1, b1, w2, b2, const, out):
    at, width = const_slices()
    rows = nc.dram_tensor("rows", [N, C], F32, kind="Internal").ap()
    parts = nc.dram_tensor("parts", [2 * N + P, C], F32, kind="Internal").ap()
    with ExitStack() as whole:
        def sb(ctx, name, shape, dt=F32):
            return ctx.enter_context(nc.sbuf_tensor(name, shape, dt))

        consts = sb(whole, "consts", [P, width])
        lg = sb(whole, "lg", [P, NT, E])
        wts = sb(whole, "wts", [P, 2, NT])
        ids = sb(whole, "ids", [P, SLOTS], I32)
        dst = sb(whole, "dst", [P, SLOTS], I32)
        tile_expert = sb(whole, "tile_expert", [P, SLOTS], I32)
        acc = sb(whole, "acc", [P, NT, C])
        with ExitStack() as until_combine:
            weights = Weights(nc, until_combine, w1, w2)
            with ExitStack() as ctx:
                graph_layer(nc, ctx, x, adj, adj_rows, w, gate_w, gate_b, const, rows, consts, at, acc, lg,
                            weights)
            weights.w2r = weights.tensor("w2r", KF, C)
            b1a = sb(until_combine, "b1a", [P, E, F])
            b1_loaded = until_combine.enter_context(nc.semaphore("b1_loaded"))
            with ExitStack() as ctx:
                route(nc, ctx, weights, b1, consts, at, lg, wts, ids, dst, tile_expert, b1a, b1_loaded)
            with ExitStack() as ctx:
                experts(nc, ctx, b1a, b1_loaded, b2, rows, parts, consts, at, ids, dst, tile_expert, weights)
        with ExitStack() as ctx:
            combine(nc, ctx, parts, out, acc, wts)


def constants():
    import numpy as np
    lane = np.arange(P)
    table = dict(ident=np.eye(P), before=lane[:, None] < lane[None, :], lane=lane, tile=np.arange(SLOTS),
                 expert=np.arange(E), step=P * np.arange(NT), column=1 + np.arange(CW), row=lane[:, None])
    parts = [np.broadcast_to(table[name], (P, width)) for name, width in WIDTHS.items()]
    return np.ascontiguousarray(np.concatenate(parts, 1).astype(np.float32))


def kernel(**inputs):
    import numpy as np
    import concourse.bacc as bacc
    from concourse.bass_utils import run_bass_kernel_spmd as run

    nc = bacc.Bacc("TRN2", target_bir_lowering=False, num_devices=1)
    a = {name: np.ascontiguousarray(v) for name, v in inputs.items()}
    blocks = a["adj"].T.reshape(NB, SUB, P, NB, BW).transpose(0, 3, 2, 1, 4)
    arrays = {
        "x_in": a["x"], "adj_in": np.ascontiguousarray(blocks), "adj_rows_in": a["adj"],
        "w_in": a["L0_gnn_w"],
        "gate_w_in": a["L0_ffn_gate_w"], "gate_b_in": a["L0_ffn_gate_b"], "w1_in": a["L0_ffn_w1"],
        "b1_in": a["L0_ffn_b1"], "w2_in": a["L0_ffn_w2"], "b2_in": a["L0_ffn_b2"], "const_in": constants(),
    }
    args = [nc.dram_tensor(name, v.shape, mybir.dt.from_np(v.dtype), kind="ExternalInput").ap()
            for name, v in arrays.items()]
    args.append(nc.dram_tensor("out_0", (N, C), F32, kind="ExternalOutput").ap())
    graph_then_experts(nc, *args)
    r = run(nc, [arrays], core_ids=[0])
    return r.results[0]["out_0"]
```
